# Optimizing a Trainium2 kernel written in Bass

```python
import numpy as np
import jax
import jax.numpy as jnp

def _softmax(x, axis=-1):
    return jax.nn.softmax(x, axis=axis)

def _gelu(x):
    return jax.nn.gelu(x, approximate=True)

def _silu(x):
    return jax.nn.silu(x)

def _sigmoid(x):
    return jax.nn.sigmoid(x)

def _layernorm(x, axis=-1, eps=1e-05):
    m = jnp.mean(x, axis=axis, keepdims=True)
    v = jnp.var(x, axis=axis, keepdims=True)
    return (x - m) / jnp.sqrt(v + eps)

def _scatter_add(tgt, idx, src, axis=0):
    return tgt.at[idx].add(src)

def _segment_sum(src, seg, n):
    return jax.ops.segment_sum(src, seg, n)
kernel_name = 'mk_sandwich_d1_jaxref_r8_37ff7d'

def setup_inputs(seed: int=0):
    np.random.seed(seed)
    _w = jnp.asarray

    def _L0_attn_setup():
        import jax, jax.numpy as jnp
        import numpy as np
        D_MODEL, D_INNER, D_STATE, D_CONV, DT_RANK = (128, 256, 16, 4, 64)
        B, T = (2, 256)

        def rmsnorm(x):
            eps = jnp.asarray(jnp.finfo(x.dtype).eps, x.dtype)
            return x * jax.lax.rsqrt(jnp.mean(jnp.square(x), axis=-1, keepdims=True) + eps)

        def silu(x):
            return x * jax.nn.sigmoid(x)

        def mamba(xn, in_proj_w, conv_w, conv_b, x_proj_w, dt_proj_w, dt_proj_b, A_log, D, out_proj_w):
            b, t, _ = xn.shape
            xz = jnp.einsum('btd,ed->bte', xn, in_proj_w)
            x_in, z = jnp.split(xz, 2, axis=-1)
            x_pad = jnp.pad(x_in, ((0, 0), (D_CONV - 1, 0), (0, 0)))
            x_conv = sum((conv_w[:, k] * x_pad[:, k:k + t, :] for k in range(D_CONV))) + conv_b
            x_conv = silu(x_conv)
            x_dbl = jnp.einsum('bte,fe->btf', x_conv, x_proj_w)
            dt_low = x_dbl[..., :DT_RANK]
            B_ssm = x_dbl[..., DT_RANK:DT_RANK + D_STATE]
            C_ssm = x_dbl[..., DT_RANK + D_STATE:]
            dt = jax.nn.softplus(jnp.einsum('btr,er->bte', dt_low, dt_proj_w) + dt_proj_b)
            A = -jnp.exp(A_log)

            def step(h, inp):
                dt_t, B_t, C_t, u_t = inp
                dA = jnp.exp(dt_t[..., None] * A)
                h = h * dA + (dt_t * u_t)[..., None] * B_t[:, None, :]
                y = jnp.einsum('bes,bs->be', h, C_t)
                return (h, y)
            tm = lambda a: jnp.swapaxes(a, 0, 1)
            h0 = jnp.zeros((b, D_INNER, D_STATE), xn.dtype)
            _, ys = jax.lax.scan(step, h0, (tm(dt), tm(B_ssm), tm(C_ssm), tm(x_conv)))
            y = tm(ys) + x_conv * D
            y = y * silu(z)
            return jnp.einsum('bte,de->btd', y, out_proj_w)
        key = jax.random.key(seed)
        ks = jax.random.split(key, 12)
        s = 0.02
        A_log = jnp.log(jnp.broadcast_to(jnp.arange(1, D_STATE + 1, dtype=jnp.float32), (D_INNER, D_STATE)))
        return {'x': jax.random.normal(ks[0], (B, T, D_MODEL), jnp.float32), 'in_proj_w': jax.random.normal(ks[1], (2 * D_INNER, D_MODEL), jnp.float32) * s, 'conv_w': jax.random.normal(ks[2], (D_INNER, D_CONV), jnp.float32) * 0.2, 'conv_b': jax.random.normal(ks[3], (D_INNER,), jnp.float32) * s, 'x_proj_w': jax.random.normal(ks[4], (DT_RANK + 2 * D_STATE, D_INNER), jnp.float32) * s, 'dt_proj_w': jax.random.normal(ks[5], (D_INNER, DT_RANK), jnp.float32) * 0.1, 'dt_proj_b': jax.random.normal(ks[6], (D_INNER,), jnp.float32) * 0.1 - 4.0, 'A_log': A_log, 'D': jax.random.normal(ks[7], (D_INNER,), jnp.float32) * s, 'out_proj_w': jax.random.normal(ks[8], (D_MODEL, D_INNER), jnp.float32) * s, 'c_fc_w': jax.random.normal(ks[9], (2 * D_MODEL, D_MODEL), jnp.float32) * s, 'c_proj_w': jax.random.normal(ks[10], (D_MODEL, 2 * D_MODEL), jnp.float32) * s}
    _L0_attn_in = _L0_attn_setup()

    def _L0_ffn_setup():
        import jax, jax.numpy as jnp
        import numpy as np
        CAPACITY_FACTOR = 1.0
        key = jax.random.key(seed)
        ks = jax.random.split(key, 5)
        B, S, D, E, F = (2, 256, 128, 8, 512)
        x = jax.random.normal(ks[0], (B, S, D), dtype=jnp.float32)
        Ws = jax.random.normal(ks[1], (D, E), dtype=jnp.float32) * (1.0 / np.sqrt(D))
        bs = jnp.zeros((E,), dtype=jnp.float32)
        W1 = jax.random.normal(ks[2], (E, D, F), dtype=jnp.float32) * (1.0 / np.sqrt(D))
        b1 = jnp.zeros((E, F), dtype=jnp.float32)
        W2 = jax.random.normal(ks[3], (E, F, D), dtype=jnp.float32) * (1.0 / np.sqrt(F))
        b2 = jnp.zeros((E, D), dtype=jnp.float32)
        return {'x': x, 'Ws': Ws, 'bs': bs, 'W1': W1, 'b1': b1, 'W2': W2, 'b2': b2}
    _L0_ffn_in = _L0_ffn_setup()
    _d = {'L0_attn_x': _L0_attn_in['x'], 'L0_attn_in_proj_w': _L0_attn_in['in_proj_w'], 'L0_attn_conv_w': _L0_attn_in['conv_w'], 'L0_attn_conv_b': _L0_attn_in['conv_b'], 'L0_attn_x_proj_w': _L0_attn_in['x_proj_w'], 'L0_attn_dt_proj_w': _L0_attn_in['dt_proj_w'], 'L0_attn_dt_proj_b': _L0_attn_in['dt_proj_b'], 'L0_attn_A_log': _L0_attn_in['A_log'], 'L0_attn_D': _L0_attn_in['D'], 'L0_attn_out_proj_w': _L0_attn_in['out_proj_w'], 'L0_attn_c_fc_w': _L0_attn_in['c_fc_w'], 'L0_attn_c_proj_w': _L0_attn_in['c_proj_w'], 'L0_ffn_Ws': _L0_ffn_in['Ws'], 'L0_ffn_bs': _L0_ffn_in['bs'], 'L0_ffn_W1': _L0_ffn_in['W1'], 'L0_ffn_b1': _L0_ffn_in['b1'], 'L0_ffn_W2': _L0_ffn_in['W2'], 'L0_ffn_b2': _L0_ffn_in['b2']}
    _x0 = _d['L0_attn_x']
    _d['L0_attn_x'] = jax.random.normal(jax.random.fold_in(jax.random.key(seed), 1), (2, 1024, 128), dtype=_x0.dtype)
    del _x0
    return _d

def reference(L0_attn_x, L0_attn_in_proj_w, L0_attn_conv_w, L0_attn_conv_b, L0_attn_x_proj_w, L0_attn_dt_proj_w, L0_attn_dt_proj_b, L0_attn_A_log, L0_attn_D, L0_attn_out_proj_w, L0_attn_c_fc_w, L0_attn_c_proj_w, L0_ffn_Ws, L0_ffn_bs, L0_ffn_W1, L0_ffn_b1, L0_ffn_W2, L0_ffn_b2):

    def _L0_attn_ref(x, in_proj_w, conv_w, conv_b, x_proj_w, dt_proj_w, dt_proj_b, A_log, D, out_proj_w, c_fc_w, c_proj_w):
        import jax, jax.numpy as jnp
        import numpy as np
        D_MODEL, D_INNER, D_STATE, D_CONV, DT_RANK = (128, 256, 16, 4, 64)
        B, T = (2, 256)

        def rmsnorm(x):
            eps = jnp.asarray(jnp.finfo(x.dtype).eps, x.dtype)
            return x * jax.lax.rsqrt(jnp.mean(jnp.square(x), axis=-1, keepdims=True) + eps)

        def silu(x):
            return x * jax.nn.sigmoid(x)

        def mamba(xn, in_proj_w, conv_w, conv_b, x_proj_w, dt_proj_w, dt_proj_b, A_log, D, out_proj_w):
            b, t, _ = xn.shape
            xz = jnp.einsum('btd,ed->bte', xn, in_proj_w)
            x_in, z = jnp.split(xz, 2, axis=-1)
            x_pad = jnp.pad(x_in, ((0, 0), (D_CONV - 1, 0), (0, 0)))
            x_conv = sum((conv_w[:, k] * x_pad[:, k:k + t, :] for k in range(D_CONV))) + conv_b
            x_conv = silu(x_conv)
            x_dbl = jnp.einsum('bte,fe->btf', x_conv, x_proj_w)
            dt_low = x_dbl[..., :DT_RANK]
            B_ssm = x_dbl[..., DT_RANK:DT_RANK + D_STATE]
            C_ssm = x_dbl[..., DT_RANK + D_STATE:]
            dt = jax.nn.softplus(jnp.einsum('btr,er->bte', dt_low, dt_proj_w) + dt_proj_b)
            A = -jnp.exp(A_log)

            def step(h, inp):
                dt_t, B_t, C_t, u_t = inp
                dA = jnp.exp(dt_t[..., None] * A)
                h = h * dA + (dt_t * u_t)[..., None] * B_t[:, None, :]
                y = jnp.einsum('bes,bs->be', h, C_t)
                return (h, y)
            tm = lambda a: jnp.swapaxes(a, 0, 1)
            h0 = jnp.zeros((b, D_INNER, D_STATE), xn.dtype)
            _, ys = jax.lax.scan(step, h0, (tm(dt), tm(B_ssm), tm(C_ssm), tm(x_conv)))
            y = tm(ys) + x_conv * D
            y = y * silu(z)
            return jnp.einsum('bte,de->btd', y, out_proj_w)
        x = x + mamba(rmsnorm(x), in_proj_w, conv_w, conv_b, x_proj_w, dt_proj_w, dt_proj_b, A_log, D, out_proj_w)
        h = rmsnorm(x)
        h = jnp.square(jax.nn.relu(jnp.einsum('btd,ed->bte', h, c_fc_w)))
        x = x + jnp.einsum('bte,de->btd', h, c_proj_w)
        return x

    def _L0_ffn_ref(x, Ws, bs, W1, b1, W2, b2):
        import jax, jax.numpy as jnp
        import numpy as np
        CAPACITY_FACTOR = 1.0
        B, S, D = x.shape
        E = Ws.shape[1]
        N = B * S
        k = int(CAPACITY_FACTOR * N / E)
        xf = x.reshape(N, D)
        route_prob = jax.nn.softmax(xf @ Ws + bs, axis=-1).T
        route_vals, routes = jax.lax.top_k(route_prob, k)
        xin = xf[routes]
        h = jax.nn.gelu(jnp.einsum('ekd,edf->ekf', xin, W1) + b1[:, None, :])
        out = jnp.einsum('ekf,efd->ekd', h, W2) + b2[:, None, :]
        out = out * route_vals[..., None]
        final = jnp.zeros((N, D), dtype=x.dtype).at[routes.reshape(-1)].add(out.reshape(-1, D))
        return final.reshape(B, S, D)
    x = L0_attn_x
    x = x + _layernorm(_L0_attn_ref(_layernorm(x, axis=-1), L0_attn_in_proj_w, L0_attn_conv_w, L0_attn_conv_b, L0_attn_x_proj_w, L0_attn_dt_proj_w, L0_attn_dt_proj_b, L0_attn_A_log, L0_attn_D, L0_attn_out_proj_w, L0_attn_c_fc_w, L0_attn_c_proj_w), axis=-1)
    x = x + _layernorm(_L0_ffn_ref(_layernorm(x, axis=-1), L0_ffn_Ws, L0_ffn_bs, L0_ffn_W1, L0_ffn_b1, L0_ffn_W2, L0_ffn_b2), axis=-1)
    return x

_drawn_inputs = setup_inputs


def setup_inputs(seed=0):
    import zlib

    import numpy as np

    out = dict(_drawn_inputs(seed))
    spreads = {'L0_ffn_bs': (0.0, 0.1), 'L0_ffn_b1': (0.0, 0.1), 'L0_ffn_b2': (0.0, 0.1)}
    factors = {'L0_attn_in_proj_w': 8.0,
     'L0_attn_conv_w': 6.706,
     'L0_attn_conv_b': 8.0,
     'L0_attn_x_proj_w': 8.0,
     'L0_attn_dt_proj_w': 8.0,
     'L0_attn_dt_proj_b': 8.0,
     'L0_attn_A_log': 8.0,
     'L0_attn_D': 200.0,
     'L0_attn_out_proj_w': 8.0,
     'L0_attn_c_fc_w': 64.0,
     'L0_attn_c_proj_w': 64.0}
    for name, (base, spread) in spreads.items():
        noise = np.random.default_rng([zlib.crc32(name.encode()), seed]).standard_normal(out[name].shape)
        drawn = base * np.exp(spread * noise) if base else spread * noise
        out[name] = jnp.asarray(drawn.astype(out[name].dtype))
    for name, factor in factors.items():
        out[name] = (out[name] * factor).astype(out[name].dtype)
    return out
```

```python
from contextlib import ExitStack

import concourse.bass as bass
from concourse import mybir

ALU = mybir.AluOpType
ACT = mybir.ActivationFunctionType
F32 = mybir.dt.float32
BF16 = mybir.dt.bfloat16
I32 = mybir.dt.int32
AX_X = mybir.AxisListType.X

LN_EPS = 1e-05
RMS_EPS = 2.0 ** -23
ONE_BITS = 30


def sandwich_kernel(nc, x, in_w_t, conv_w, conv_b, xp_w_t, dt_w_t, dt_b, a_log, d_skip, out_w_t,
                    fc_w_t, pr_w_t, ws, bs, w1, b1, w2, b2, out):
    B, T, DM = x.shape
    DI = conv_w.shape[0]
    NS = a_log.shape[1]
    TAPS = conv_w.shape[1]
    R = dt_w_t.shape[0]
    E, _, F = w1.shape
    P = 128
    N = B * T
    NT = N // P
    TB = T // P
    CH = 512
    HC = T // CH
    CT = CH // P
    H = DI // P
    XR = R + 2 * NS
    LO = 16
    KSEL = N // E
    SH = KSEL // P
    HI = KSEL // LO
    LOW_HI = P // LO
    FK = F // P
    FH = fc_w_t.shape[1] // P
    RING = 4
    STEP_BITS = 3
    NTHR = 2 ** STEP_BITS - 1
    ROUNDS = ONE_BITS // STEP_BITS
    CLEARED = 48
    NLOADS = 15
    ZB = (6, 2)
    DTB = (4, 6)
    assert E * HI == P and DM == P and H == 2 and HC == 2 and TB == 8 and E * NT == P and SH == 2 and FH == 2
    assert NS % RING == 0 and ROUNDS * STEP_BITS == ONE_BITS

    bc_dram = nc.dram_tensor("bc_rows", (B, 2, NS, T), F32, kind="Internal").ap()
    ROW = DM + E
    xb_dram = nc.dram_tensor("ffn_in_rows", (N, ROW), F32, kind="Internal").ap()
    fin_dram = nc.dram_tensor("ffn_sum_rows", (N, DM), F32, kind="Internal").ap()

    with ExitStack() as ctx:
        def sb(name, shape, dt=F32):
            return ctx.enter_context(nc.sbuf_tensor(name, shape, dt))

        def sem(name):
            return ctx.enter_context(nc.semaphore(name))

        win = sb("win", [P, 2 * DI])
        convw = sb("convw", [P, H, TAPS])
        xpw = sb("xpw", [P, H, XR])
        dtw = sb("dtw", [R, DI])
        outw = sb("outw", [P, H, DM])
        fcw = sb("fcw", [P, FH * P])
        prw = sb("prw", [P, FH, DM])
        wsr = sb("wsr", [P, E])
        bsr = sb("bsr", [P, E])
        b2r = sb("b2r", [P, E, DM])
        NB1 = E * FK
        vrows = sb("vrows", [NB1 + 6, P])
        vcol = sb("vcol", [P, NB1 + 6])
        alog = sb("alog", [P, H, NS])
        aexp = sb("aexp", [P, H, NS])
        aneg = sb("aneg", [P, H, NS])
        ident = sb("ident", [P, P])
        diagd = sb("diagd", [P, H, P])
        expn = sb("expn", [P, 2 * CT])
        ones_b = sb("ones_b", [P, P], BF16)
        earlier = sb("earlier_token", [P, P], BF16)
        iota_p = sb("iota_p", [P, 1], I32)
        iota_pf = sb("iota_pf", [P, 1])
        iota_n = sb("iota_n", [P, 2 * LO], I32)
        iota_b = sb("iota_b", [P, 2 * LO], BF16)
        grp = sb("grp", [P, 3], I32)
        grpf = sb("grpf", [P, 3])
        of_expert = sb("of_expert", [P, E])
        of_slot8 = sb("of_slot8", [P, LOW_HI])
        of_half = sb("of_half", [P, E, SH])
        fresh = sb("fresh", [P, E, NT])
        jrow = sb("jrow", [P, NTHR + 1], I32)
        jbits = sb("jbits", [P, ROUNDS, NTHR + 1], I32)
        zero = sb("zero", [P, P])

        X = sb("X", [P, NT, DM])
        XA = sb("XA", [P, NT, DM])
        LG = sb("LG", [P, E, NT])
        XC = sb("XC", [P, H, T])
        SZ = sb("SZ", [P, H, T])
        DT = sb("DT", [P, H, T])
        DU = sb("DU", [P, H, T])
        DA = sb("DA", [P, 2, H, T])
        DB = sb("DB", [P, RING, H, T])
        G = sb("G", [P, 2, H, T])
        BC = sb("BC", [P, RING, 2, T])
        bst = sb("bst", [P, HC, CT, 6])
        mv = sb("mv", [P, HC, CT, 2])
        vv = sb("vv", [P, HC, 2, CT])
        rs = sb("rs", [P, HC, 2, CT])
        xn = sb("xn", [P, HC, CT, DM])
        xnT = sb("xnT", [P, HC, CH])
        xin = sb("xin", [P, H, TAPS - 1 + T])
        dbl = sb("dbl", [XR, HC, CH])
        cacc = G[:, 0, :, :].rearrange("p h (c n) -> p c h n", c=HC)
        tmp1 = G[:, 1, :, :].rearrange("p h (c n) -> p c h n", c=HC)
        tmp2 = G[:, 0, :, :].rearrange("p h (c n) -> p c h n", c=HC)
        DBf = DB[:, :, :, :].rearrange("p r h t -> p (r h t)")

        def lent(ring, at, *dims):
            n = 1
            for d in dims:
                n *= d
            names = " ".join(f"d{i}" for i in range(len(dims)))
            kw = {f"d{i}": d for i, d in enumerate(dims)}
            v = ring[:, at:at + n]
            return v.rearrange(f"p ({names}) -> p {names}", **kw) if len(dims) > 1 else v

        def view(at, *dims):
            return lent(DBf, at, *dims)

        x2 = view(0, HC, CT, DM)
        hn = view(1024, HC, CT, DM)
        hnT = view(2048, HC, CH)
        rel = view(3072, HC, FH, CH)
        xb = view(5120, HC, CT, DM)
        xbT = view(6144, HC, CH)
        sq = view(7168, HC, CT, DM)
        ssq = sb("ssq", [P, HC, CT])
        vv2 = sb("vv2", [P, HC, CT])
        rs2 = sb("rs2", [P, HC, CT])
        mx = sb("mx", [P, NT])
        sm = sb("sm", [P, NT])
        rsm = sb("rsm", [P, NT])
        PT = sb("PT", [P, NT, E])
        base = sb("base", [P, E], I32)
        thr = sb("thr", [P, NTHR + 1, E], I32)
        ge = sb("ge", [P, 2, E, NT], BF16)
        sel = sb("sel", [P, E, NT], BF16)
        tot = sb("tot", [P, E, NT])
        run = sb("run", [P, E, NT])
        need = sb("need", [P, E])
        rank = sb("rank", [P, E, NT])
        slot = sb("slot", [P, E, NT], I32)
        shi = sb("slot_high_i", [P, E, NT], I32)
        slo = sb("slot_low_i", [P, E, NT], I32)
        hib = sb("slot_high", [P, E, NT], BF16)
        lob = sb("slot_low", [P, E, NT], BF16)
        Gb = G[:, :, :, :].rearrange("p r h t -> p (r h t)").bitcast(BF16)
        DAf = DA[:, :, :, :].rearrange("p r h t -> p (r h t)")
        ohh = lent(Gb, 0, NT, E, HI)
        ohl = lent(Gb, NT * E * HI, NT, E, LO)
        ohv = lent(Gb, NT * E * (HI + LO), NT, 2, E, LO)
        reach = lent(DAf.bitcast(BF16), 0, NT, NTHR, E)
        dm = sb("dm", [P, 2, E, LO])
        dv = sb("dv", [P, 2, LO])
        tok = sb("tok", [P, LO])
        spread = sb("spread", [P, LOW_HI, LO])
        idx = sb("idx", [P, E + 2, SH], I32)
        gidx = [sb(f"gidx{i}", [P, SH], I32) for i in range(2)]
        sidx = [sb(f"sidx{i}", [P, SH], I32) for i in range(2)]
        prob = [sb(f"prob{i}", [P, SH]) for i in range(2)]
        w1s = lent(DAf, 1024, 2, F)
        w2s = lent(DAf, 2048, 2, FK, DM)
        xi = [view(i * 288, SH, ROW) for i in range(2)]
        xiT = [view(7168 + i * 256, KSEL) for i in range(2)]
        hT = [view(1024 + i * 1024, FK, KSEL) for i in range(2)]
        ost = [view(3072 + i * 256, SH, DM) for i in range(2)]
        NC5 = NT // CT
        bst5 = sb("bst5", [P, NC5, CT, 6])
        mv5 = sb("mv5", [P, NC5, CT, 2])
        vv5 = sb("vv5", [P, NC5, CT])
        rs5 = sb("rs5", [P, NC5, CT])
        nb5 = sb("nb5", [P, NC5, CT])
        fin = view(0, NT // CT, CT, DM)
        res = view(2048, NT // CT, CT, DM)

        PS = ctx.enter_context(nc.psum_tensor("PS", [P, 8, CH], F32))
        Y = PS[:, 0:4, :].rearrange("p (h c) n -> p h (c n)", h=H)

        s_x = sem("x_loaded"); s_w = sem("weights_loaded"); 
        s_const = sem("constants"); s_id = sem("identity_made"); s_vt = sem("vector_rows_turned"); s_vc = sem("vector_columns")
        s_ae = sem("a_exp"); s_an = sem("a_negated"); s_dd = sem("skip_diagonal")
        s_mv = sem("ln1_stats"); s_rs = sem("ln1_scales"); s_xn = sem("normed"); s_xtp = sem("normed_turned"); s_xt = sem("normed_t")
        s_xip = sem("x_in_product"); s_xi = sem("x_in"); s_zp = sem("z_product"); s_z = sem("gate_silu")
        s_cv = sem("convolved"); s_xc = sem("x_conv"); s_dbp = sem("x_dbl_product"); s_db = sem("x_dbl")
        s_bw = [sem(f"bc_stored{i}") for i in range(HC)]
        s_dtp = sem("dt_product"); s_ex = sem("softplus_parts"); s_e1 = sem("softplus_head"); s_sp = sem("softplus_tail")
        s_du = sem("dt_u")
        s_bc = [sem(f"bc_slot_loaded{i}") for i in range(RING)]
        s_dA = sem("decay"); s_dB = sem("input_term"); s_h = sem("states"); s_g = sem("states_times_c"); s_y = sem("y_summed")
        s_yi = sem("y_started"); s_yg = sem("y_gated")
        s_op = sem("out_product"); s_x2 = sem("x2"); s_sq = sem("x2_squares"); s_r2 = sem("rms2_scales"); s_hn = sem("hn")
        s_htp = sem("hn_turned"); s_ht = sem("hn_t"); s_fp = sem("fc_product"); s_re = sem("relu"); s_hd = sem("relu_squared")
        s_pp = sem("proj_product"); s_st3 = sem("ln2_stats"); s_r3 = sem("ln2_scales"); s_st4 = sem("ln3_stats"); s_r4 = sem("ln3_scales")
        s_xb = sem("ffn_in"); s_xw = [sem(f"ffn_in_stored{i}") for i in range(HC)]
        s_xbp = sem("ffn_in_turned"); s_xbt = sem("ffn_in_t"); s_lp = sem("logit_product"); s_lg = sem("logits")
        s_sub = sem("logits_less_max"); s_pe = sem("exp_logits"); s_pr = sem("probs"); s_vp = sem("probs_turned"); s_v = sem("probs_rows")
        s_cn = sem("counts"); s_ct = sem("counts_summed"); s_rw = sem("row_sums"); s_rt = sem("rows_summed")
        s_slot = sem("slots"); s_stp = sem("slots_turned"); 
        s_idx = sem("indices")
        s_gt = [sem(f"gathered{i}") for i in range(2)]
        s_wl = [sem(f"expert_weights{i}") for i in range(2)]
        s_xtu = sem("gathered_turned"); s_xit = sem("gathered_t"); s_hp = sem("w1_product"); s_ge = sem("gelu")
        s_o2 = sem("w2_product"); s_os = sem("expert_out"); s_sc = sem("scattered")
        s_fl = [sem(f"ffn_sum_loaded{i}") for i in range(NC5)]
        s_st5 = sem("ln4_stats"); s_r5 = sem("ln4_scales"); s_res = sem("result"); s_out = sem("stored"); s_pt = sem("probs_by_token"); s_pw = sem("probs_stored"); s_nm = sem("ln4_normed"); s_oh = sem("one_hots"); s_dp = sem("slot_tokens"); s_spd = sem("slot_tokens_spread"); s_ixp = sem("index_product"); s_nb = sem("ln4_shifts")
        s_past = sem("past_a_wait"); s_th = sem("thresholds"); s_gi = sem("gather_indices"); s_si = sem("scatter_indices"); s_v5 = sem("ln4_variances"); s_ab = sem("softplus_abs"); s_eu = sem("softplus_exp")

        convb = vcol[:, NB1:NB1 + 2]
        dtb = vcol[:, NB1 + 2:NB1 + 4]
        dcol = vcol[:, NB1 + 4:NB1 + 6]
        x_rows = x.rearrange("b (t p) d -> p (b t) d", p=P)
        out_rows = out.rearrange("b (t p) d -> p (b t) d", p=P)

        block = ctx.enter_context(nc.Block())

        @block.sync
        def _(sp):
            sp.dma_start(X[:, :, :], x_rows).then_inc(s_x, 16)
            loads = [
                (win[:, :], in_w_t), (vrows[0:NB1, :], b1.rearrange("e (k p) -> (e k) p", p=P)),
                (vrows[NB1:NB1 + 2, :], conv_b.rearrange("(h p) -> h p", p=P)),
                (vrows[NB1 + 2:NB1 + 4, :], dt_b.rearrange("(h p) -> h p", p=P)),
                (vrows[NB1 + 4:NB1 + 6, :], d_skip.rearrange("(h p) -> h p", p=P)),
                (convw[:, :, :], conv_w.rearrange("(h p) k -> p h k", p=P)),
                (xpw[:, :, :], xp_w_t.rearrange("(h p) f -> p h f", p=P)),
                (dtw[:, :], dt_w_t), (alog[:, :, :], a_log.rearrange("(h p) s -> p h s", p=P)),
                (outw[:, :, :], out_w_t.rearrange("(h p) d -> p h d", p=P)),
                (fcw[:, :], fc_w_t), (prw[:, :, :], pr_w_t.rearrange("(h p) d -> p h d", p=P)),
                (wsr[:, :], ws), (bsr[:, :], bs.rearrange("(a e) -> a e", a=1).broadcast_to([P, E])),
                (b2r[:, :, :], b2.unsqueeze(0).broadcast_to([P, E, DM])),
            ]
            assert len(loads) == NLOADS
            for dst, src in loads:
                sp.dma_start(dst, src).then_inc(s_w, 16)
            with sp.Fori(0, B) as b:
                for hc in range(HC):
                    sp.wait_ge(s_db, b * HC + hc + 1)
                    sp.dma_start(bc_dram[b, :, :, hc * CH:(hc + 1) * CH].rearrange("w s n -> (w s) n"),
                                 dbl[R:XR, hc, :]).then_inc(s_bw[hc], 16)
                for hc in range(HC):
                    sp.wait_ge(s_bw[hc], b * 16 + 16)
                sp.sem_inc(s_past, 1)
                with sp.Fori(0, NS // RING) as it:
                    s = it * RING
                    for i in range(RING):
                        sp.wait_ge(s_dB, b * NS + s + i + 1)
                        sp.wait_ge(s_g, b * NS + s + i + 1)
                        sp.dma_start(BC[:, i, :, :],
                                     bc_dram[b, :, s + i, :].unsqueeze(0).broadcast_to([P, 2, T])
                                     ).then_inc(s_bc[i], 16)
                for hc in range(HC):
                    sp.wait_ge(s_xb, b * HC + hc + 1)
                    sp.dma_start(xb_dram.rearrange("(t p) d -> p t d", p=P)[:, bass.ds(b * TB + hc * CT, CT), 0:DM],
                                 xb[:, hc, :, :]).then_inc(s_xw[hc], 16)
            sp.wait_ge(s_pt, 1)
            sp.dma_start(xb_dram.rearrange("(t p) d -> p t d", p=P)[:, :, DM:ROW], PT[:, :, :]).then_inc(s_pw, 16)
            with sp.Fori(0, E // 2) as it:
                e = it * 2
                for u in range(2):
                    sp.wait_ge(s_o2, e + u + 1)
                    sp.dma_start(w1s[:, u, :], w1[e + u, :, :]).then_inc(s_wl[u], 16)
                    sp.dma_start(w2s[:, u, :, :], w2[e + u, :, :].rearrange("(k p) d -> p k d", p=P)
                                 ).then_inc(s_wl[u], 16)
            sp.wait_ge(s_sc, CLEARED + 32 * E)
            for c in range(NC5):
                sp.dma_start(fin[:, c, :, :], fin_dram.rearrange("(t p) d -> p t d", p=P)[:, c * CT:(c + 1) * CT, :]
                             ).then_inc(s_fl[c], 16)
            for c in range(NC5):
                sp.wait_ge(s_res, c + 1)
                sp.dma_start(out_rows[:, c * CT:(c + 1) * CT, :], res[:, c, :, :]).then_inc(s_out, 16)
            sp.wait_ge(s_out, 16 * NC5)

        @block.gpsimd
        def _(pool):
            pool.sem_inc(s_dB, RING)
            pool.memset(zero[:, :], 0.0)
            pool.memset(expn[:, :], -0.5)
            pool.memset(xin[:, :, 0:TAPS - 1], 0.0)
            pool.memset(ident[:, :], 0.0)
            pool.memset(ones_b[:, :], 1.0)
            pool.memset(fresh[:, :, :], 1.0)
            pool.drain().then_inc(s_const, 1)
            for t in range(0, NT, 6):
                n = min(6, NT - t)
                pool.dma_start(fin_dram.rearrange("(t p) d -> p t d", p=P)[:, t:t + n, :],
                               zero[:, :].unsqueeze(1).broadcast_to([P, n, DM])).then_inc(s_sc, 16)
            pool.affine_select(out=ident[:, :], in_=ident[:, :], compare_op=ALU.not_equal, fill=1.0, base=0,
                               pattern=[[-1, P]], channel_multiplier=1).then_inc(s_id, 1)
            pool.affine_select(out=earlier[:, :], in_=ones_b[:, :], compare_op=ALU.is_ge, fill=0.0, base=-1,
                               pattern=[[1, P]], channel_multiplier=-1)
            pool.memset(fresh[:, :, 0:1], 0.0)
            pool.iota(iota_p[:, :], pattern=[[1, 1]], base=0, channel_multiplier=1)
            pool.iota(iota_n[:, :], pattern=[[1, 2 * LO]], base=0, channel_multiplier=0)
            pool.iota(jrow[:, :], pattern=[[1, NTHR + 1]], base=0, channel_multiplier=0)
            pool.wait_ge(s_sc, CLEARED)
            pool.drain().then_inc(s_const, 1)
            with pool.Fori(0, B) as b:
                for hc in range(HC):
                    pool.wait_ge(s_mv, b * HC + hc + 1)
                    pool.sem_inc(s_past, 1)
                    pool.tensor_scalar(vv[:, hc, 0, :], mv[:, hc, :, 1], LN_EPS, None, ALU.add)
                    pool.tensor_scalar(vv[:, hc, 1, :], mv[:, hc, :, 1], 1.0 + RMS_EPS, LN_EPS * RMS_EPS, ALU.mult, ALU.add)
                    pool.drain()
                    pool.tensor_tensor(rs[:, hc, :, :].rearrange("p a t -> p (a t)"),
                                       vv[:, hc, :, :].rearrange("p a t -> p (a t)"), expn[:, :],
                                       ALU.pow).then_inc(s_rs, 1)
                for hc in range(HC):
                    n = slice(hc * CH, (hc + 1) * CH)
                    pool.wait_ge(s_e1, b * HC + hc + 1)
                    pool.tensor_tensor(tmp1[:, hc, :, :], DU[:, :, n], tmp1[:, hc, :, :], ALU.subtract)
                    pool.drain()
                    pool.tensor_tensor(tmp1[:, hc, :, :], tmp1[:, hc, :, :], tmp2[:, hc, :, :], ALU.add).then_inc(s_sp, 1)
                pool.wait_ge(s_du, b * HC + HC)
                pool.wait_ge(s_lg, b * HC + 1)
                pool.sem_inc(s_past, 1)
                with pool.Fori(0, NS // RING) as it:
                    s = it * RING
                    for i in range(RING):
                        pool.wait_ge(s_bc[i], (b * (NS // RING)) * 16 + s * (16 // RING) + 16)
                        pool.wait_ge(s_g, b * NS + s + i + 1)
                        pool.tensor_tensor(DB[:, i, :, :], DU[:, :, :],
                                           BC[:, i, 0, :].unsqueeze(1).broadcast_to([P, H, T]), ALU.mult
                                           ).then_inc(s_dB, 1)
                for hc in range(HC):
                    pool.wait_ge(s_sq, b * HC + hc + 1)
                    pool.sem_inc(s_past, 1)
                    pool.tensor_scalar(vv2[:, hc, :], ssq[:, hc, :], RMS_EPS, None, ALU.add)
                    pool.drain()
                    pool.tensor_tensor(rs2[:, hc, :], vv2[:, hc, :], expn[:, 0:CT], ALU.pow).then_inc(s_r2, 1)
                for stats, scales in ((s_st3, s_r3), (s_st4, s_r4)):
                    for hc in range(HC):
                        pool.wait_ge(stats, b * HC + hc + 1)
                        pool.sem_inc(s_past, 1)
                        pool.tensor_scalar(vv2[:, hc, :], mv[:, hc, :, 1], LN_EPS, None, ALU.add)
                        pool.drain()
                        pool.tensor_tensor(rs2[:, hc, :], vv2[:, hc, :], expn[:, 0:CT], ALU.pow).then_inc(scales, 1)


            pool.wait_ge(s_pr, 1)
            pool.tensor_copy(PT[:, :, :], LG[:, :, :].rearrange("p e t -> p t e")).then_inc(s_pt, 1)

            def gather(u, n):
                pool.wait_ge(s_gi, n)
                pool.sem_inc(s_past, 1)
                for j in range(SH):
                    pool.indirect_dma_start(
                        out=xi[u][:, j, :], out_offset=None, in_=xb_dram[:, :],
                        in_offset=bass.IndirectOffsetOnAxis(ap=gidx[u][:, j:j + 1], axis=0)).then_inc(s_gt[u], 16)

            def scatter(e, u):
                pool.wait_ge(s_os, e + (u + 3))
                pool.wait_ge(s_sc, e * 32 + (u * 32 + CLEARED))
                pool.sem_inc(s_past, 1)
                for j in range(SH):
                    pool.indirect_dma_start(
                        out=fin_dram[:, :], out_offset=bass.IndirectOffsetOnAxis(ap=sidx[u][:, j:j + 1], axis=0),
                        in_=ost[u][:, j, :], in_offset=None, compute_op=ALU.add).then_inc(s_sc, 16)

            for hc in range(HC):
                pool.wait_ge(s_xw[hc], 16 * B)
            pool.wait_ge(s_sc, CLEARED)
            pool.wait_ge(s_pw, 16)
            for u in range(2):
                gather(u, u + 1)
            with pool.Fori(0, E // 2 - 1) as it:
                e = it * 2
                for u in range(2):
                    gather(u, e + (u + 3))
                for u in range(2):
                    scatter(e, u)
            for u in range(2):
                scatter(E - 2, u)
            for c in range(NT // CT):
                pool.wait_ge(s_st5, c + 1)
                pool.tensor_scalar(vv5[:, c, :], mv5[:, c, :, 1], LN_EPS, None, ALU.add).then_inc(s_v5, 1)
                pool.wait_ge(s_v5, c + 1)
                pool.tensor_tensor(rs5[:, c, :], vv5[:, c, :], expn[:, 0:CT], ALU.pow).then_inc(s_r5, 1)

        @block.scalar
        def _(act):
            act.sem_inc(s_xit, 2)
            act.sem_inc(s_ge, 2)
            act.wait_ge(s_w, 16 * NLOADS)
            act.activation(aexp[:, :, :], alog[:, :, :], ACT.Exp).then_inc(s_ae, 1)
            with act.Fori(0, B) as b:
                for hc in range(HC):
                    act.wait_ge(s_xtp, b * HC + hc + 1)
                    act.copy(xnT[:, hc, :], PS[:, hc, :]).then_inc(s_xt, 1)
                for hc in range(HC):
                    act.wait_ge(s_xip, b * HC + hc + 1)
                    act.copy(xin[:, :, TAPS - 1 + hc * CH:TAPS - 1 + (hc + 1) * CH],
                             PS[:, 2 + 2 * hc:4 + 2 * hc, :]).then_inc(s_xi, 1)
                act.wait_ge(s_vc, 1)
                for hc in range(HC):
                    n = slice(hc * CH, (hc + 1) * CH)
                    act.wait_ge(s_zp, b * HC + hc + 1)
                    act.activation(SZ[:, :, n], PS[:, ZB[hc]:ZB[hc] + 2, :], ACT.Silu).then_inc(s_z, 1)
                for hc in range(HC):
                    n = slice(hc * CH, (hc + 1) * CH)
                    act.wait_ge(s_cv, b * HC + hc + 1)
                    for h in range(H):
                        last = act.activation(XC[:, h, n], cacc[:, hc, h, :], ACT.Silu, bias=convb[:, h:h + 1])
                    last.then_inc(s_xc, 1)
                for hc in range(HC):
                    act.wait_ge(s_dbp, b * HC + hc + 1)
                    act.copy(dbl[:, hc, :], PS[0:XR, hc, :]).then_inc(s_db, 1)
                for hc in range(HC):
                    n = slice(hc * CH, (hc + 1) * CH)
                    act.wait_ge(s_dtp, b * HC + hc + 1)
                    for h in range(H):
                        act.activation(tmp2[:, hc, h, :], PS[:, DTB[hc] + h, :], ACT.Abs, bias=dtb[:, h:h + 1])
                        last = act.activation(DT[:, h, n], PS[:, DTB[hc] + h, :], ACT.Relu, bias=dtb[:, h:h + 1])
                    last.then_inc(s_ab, 1)
                    act.wait_ge(s_ab, b * HC + hc + 1)
                    act.activation(DU[:, :, n], tmp2[:, hc, :, :], ACT.Exp, scale=-1.0).then_inc(s_eu, 1)
                    act.wait_ge(s_eu, b * HC + hc + 1)
                    act.activation(tmp2[:, hc, :, :], DU[:, :, n], ACT.Ln, bias=1.0).then_inc(s_ex, 1)
                act.wait_ge(s_du, b * HC + HC)
                act.wait_ge(s_an, 1)
                with act.Fori(0, NS // RING) as it:
                    s = it * RING
                    for i in range(RING):
                        act.wait_ge(s_h, b * NS + s + (i + 1))
                        for h in range(H):
                            last = act.activation(DA[:, i % 2, h, :], DT[:, h, :], ACT.Exp,
                                                  scale=aneg[:, h, bass.ds(s + i, 1)])
                        last.then_inc(s_dA, 1)
                for hc in range(HC):
                    act.wait_ge(s_x2, b * HC + hc + 1)
                    for j in range(CT):
                        last = act.activation(sq[:, hc, j, :], x2[:, hc, j, :], ACT.Square, scale=float(DM) ** -0.5,
                                              accum_out=ssq[:, hc, j:j + 1])
                    last.then_inc(s_sq, 1)
                for hc in range(HC):
                    act.wait_ge(s_htp, b * HC + hc + 1)
                    act.copy(hnT[:, hc, :], PS[:, 5 + 2 * hc, :]).then_inc(s_ht, 1)
                for hc in range(HC):
                    act.wait_ge(s_fp, b * HC + hc + 1)
                    act.activation(rel[:, hc, :, :], PS[:, 2 * hc:2 * hc + 2, :], ACT.Relu).then_inc(s_re, 1)
                for hc in range(HC):
                    act.wait_ge(s_xbp, b * HC + hc + 1)
                    act.copy(xbT[:, hc, :], PS[:, 5 + 2 * hc, :]).then_inc(s_xbt, 1)
            act.wait_ge(s_sub, 1)
            act.activation(LG[:, :, :], LG[:, :, :], ACT.Exp).then_inc(s_pe, 1)
            with act.Fori(0, E // 2) as it:
                e = it * 2
                for u in range(2):
                    act.wait_ge(s_xtu, e + (u + 1))
                    act.copy(xiT[u][:, :], PS[:, 2 + u, 0:KSEL]).then_inc(s_xit, 1)
                for u in range(2):
                    act.wait_ge(s_hp, e + (u + 1))
                    act.wait_ge(s_o2, e + (u + 1))
                    for k in range(FK):
                        last = act.activation(hT[u][:, k, :], PS[:, 4 + 2 * u + k // 2, (k % 2) * KSEL:(k % 2 + 1) * KSEL],
                                              ACT.Gelu_apprx_tanh, bias=vcol[:, bass.ds(e * FK + (u * FK + k), 1)])
                    last.then_inc(s_ge, 1)
            for c in range(NC5):
                act.wait_ge(s_nb, c + 1)
                act.wait_ge(s_r5, c + 1)
                for j in range(CT):
                    last = act.activation(fin[:, c, j, :], fin[:, c, j, :], ACT.Identity, scale=rs5[:, c, j:j + 1],
                                          bias=nb5[:, c, j:j + 1])
                last.then_inc(s_nm, 1)

        @block.vector
        def _(dve):
            dve.sem_inc(s_g, RING)
            dve.sem_inc(s_h, 2)
            dve.sem_inc(s_os, 2)
            dve.sem_inc(s_lg, 1)
            dve.wait_ge(s_vt, 1)
            dve.tensor_copy(vcol[:, :], PS[:, 7, 0:NB1 + 6]).then_inc(s_vc, 1)
            dve.wait_ge(s_vc, 1)
            for h in range(H):
                last = dve.tensor_scalar(diagd[:, h, :], ident[:, :], dcol[:, h:h + 1], None, ALU.mult)
            last.then_inc(s_dd, 1)
            dve.wait_ge(s_ae, 1)
            dve.tensor_scalar(aneg[:, :, :], aexp[:, :, :], -1.0, None, ALU.mult).then_inc(s_an, 1)
            dve.wait_ge(s_const, 2)
            dve.tensor_copy(iota_b[:, :], iota_n[:, :])
            dve.tensor_copy(iota_pf[:, :], iota_p[:, :])
            for col, shift, mask in ((0, 4, 127), (1, 0, LOW_HI - 1), (2, 3, 127)):
                dve.tensor_scalar(grp[:, col:col + 1], iota_p[:, :], shift, mask, ALU.logical_shift_right, ALU.bitwise_and)
            for r in range(ROUNDS):
                dve.tensor_scalar(jbits[:, r, :], jrow[:, :], ONE_BITS - STEP_BITS * (r + 1), None, ALU.logical_shift_left)
            dve.drain()
            dve.tensor_copy(grpf[:, :], grp[:, :])
            dve.drain()
            for dst, n, col in ((of_expert[:, :], E, 0), (of_slot8[:, :], LOW_HI, 1),
                                (of_half[:, :, :].rearrange("p e j -> p (e j)"), E * SH, 2)):
                dve.tensor_scalar(dst, iota_n[:, 0:n], grpf[:, col:col + 1], None, ALU.is_equal)
            dve.wait_ge(s_x, 16)
            with dve.Fori(0, B) as b:
                def layer_stats(rows, hc, done):
                    for j in range(CT):
                        dve.bn_stats(bst[:, hc, j, :], rows(j))
                    dve.drain()
                    for j in range(CT):
                        last = dve.bn_aggr(mv[:, hc, j, :], bst[:, hc, j, :])
                    last.then_inc(done, 1)

                for hc in range(HC):
                    layer_stats(lambda j: X[:, b * TB + (hc * CT + j), :], hc, s_mv)
                for hc in range(HC):
                    dve.wait_ge(s_rs, b * HC + hc + 1)
                    for dst, w, done in ((1, 1, s_xn), (0, 0, None)):
                        for j in range(CT):
                            t = b * TB + (hc * CT + j)
                            last = dve.tensor_scalar(xn[:, hc, j, :] if dst else XA[:, t, :], X[:, t, :],
                                                     mv[:, hc, j, 0:1], rs[:, hc, w, j:j + 1], ALU.subtract, ALU.mult)
                        if done is not None:
                            last.then_inc(done, 1)
                dve.wait_ge(s_w, 16 * NLOADS)
                dve.wait_ge(s_y, b * NS + 2)
                for hc in range(HC):
                    dve.wait_ge(s_xi, b * HC + hc + 1)
                    for k in range(TAPS):
                        for h in range(H):
                            shifted = xin[:, h, hc * CH + k:hc * CH + k + CH]
                            if k == 0:
                                last = dve.tensor_scalar(cacc[:, hc, h, :], shifted, convw[:, h, 0:1], None, ALU.mult)
                            else:
                                last = dve.scalar_tensor_tensor(cacc[:, hc, h, :], shifted, convw[:, h, k:k + 1],
                                                                cacc[:, hc, h, :], ALU.mult, ALU.add)
                        if k < TAPS - 1:
                            dve.drain()
                    last.then_inc(s_cv, 1)
                for hc in range(HC):
                    n = slice(hc * CH, (hc + 1) * CH)
                    dve.wait_ge(s_ex, b * HC + hc + 1)
                    dve.tensor_scalar(tmp1[:, hc, :, :], DU[:, :, n], 1.0, -1.0, ALU.add, ALU.add).then_inc(s_e1, 1)
                for hc in range(HC):
                    n = slice(hc * CH, (hc + 1) * CH)
                    dve.wait_ge(s_sp, b * HC + hc + 1)
                    dve.tensor_tensor(tmp1[:, hc, :, :], tmp1[:, hc, :, :], DU[:, :, n], ALU.min)
                    dve.drain()
                    dve.tensor_tensor(DT[:, :, n], DT[:, :, n], tmp1[:, hc, :, :], ALU.add)
                    dve.drain()
                    dve.tensor_tensor(DU[:, :, n], DT[:, :, n], XC[:, :, n], ALU.mult).then_inc(s_du, 1)
                with dve.Fori(0, NS // RING) as it:
                    s = it * RING
                    for i in range(RING):
                        dve.wait_ge(s_dA, b * NS + s + (i + 1))
                        dve.wait_ge(s_dB, b * NS + s + (i + 1 + RING))
                        for h in range(H):
                            last = dve.tensor_tensor_scan(DB[:, i, h, :], DA[:, i % 2, h, :], DB[:, i, h, :], 0.0,
                                                          ALU.mult, ALU.add)
                        last.then_inc(s_h, 1)
                        dve.wait_ge(s_h, b * NS + s + (i + 3))
                        dve.wait_ge(s_y, b * NS + s + (i + 1))
                        dve.tensor_tensor(G[:, i % 2, :, :], DB[:, i, :, :],
                                          BC[:, i, 1, :].unsqueeze(1).broadcast_to([P, H, T]), ALU.mult
                                          ).then_inc(s_g, 1)
                for hc in range(HC):
                    n = slice(hc * CH, (hc + 1) * CH)
                    dve.wait_ge(s_y, b * NS + (NS + 2))
                    dve.tensor_tensor(SZ[:, :, n], Y[:, :, n], SZ[:, :, n], ALU.mult).then_inc(s_yg, 1)
                for hc in range(HC):
                    ts = bass.ds(b * TB + hc * CT, CT)
                    dve.wait_ge(s_op, b * HC + hc + 1)
                    dve.tensor_tensor(x2[:, hc, :, :], XA[:, ts, :],
                                      PS[:, 4 + 2 * hc, :].rearrange("p (t d) -> p t d", t=CT), ALU.add).then_inc(s_x2, 1)
                for hc in range(HC):
                    dve.wait_ge(s_r2, b * HC + hc + 1)
                    for j in range(CT):
                        last = dve.tensor_scalar(hn[:, hc, j, :], x2[:, hc, j, :], rs2[:, hc, j:j + 1], None, ALU.mult)
                    last.then_inc(s_hn, 1)
                for hc in range(HC):
                    dve.wait_ge(s_re, b * HC + hc + 1)
                    dve.tensor_tensor(rel[:, hc, :, :], PS[:, 2 * hc:2 * hc + 2, :], rel[:, hc, :, :],
                                      ALU.mult).then_inc(s_hd, 1)
                for hc in range(HC):
                    dve.wait_ge(s_pp, b * HC + hc + 1)
                    dve.tensor_tensor(x2[:, hc, :, :], x2[:, hc, :, :],
                                      PS[:, 4 + 2 * hc, :].rearrange("p (t d) -> p t d", t=CT), ALU.add)
                    dve.drain()
                    layer_stats(lambda j: x2[:, hc, j, :], hc, s_st3)
                for hc in range(HC):
                    ts = bass.ds(b * TB + hc * CT, CT)
                    dve.wait_ge(s_r3, b * HC + hc + 1)
                    for j in range(CT):
                        dve.tensor_scalar(x2[:, hc, j, :], x2[:, hc, j, :], mv[:, hc, j, 0:1], rs2[:, hc, j:j + 1],
                                          ALU.subtract, ALU.mult)
                    dve.drain()
                    dve.tensor_tensor(XA[:, ts, :], x2[:, hc, :, :], X[:, ts, :], ALU.add)
                    dve.drain()
                    layer_stats(lambda j: XA[:, b * TB + (hc * CT + j), :], hc, s_st4)
                for hc in range(HC):
                    dve.wait_ge(s_r4, b * HC + hc + 1)
                    for j in range(CT):
                        last = dve.tensor_scalar(xb[:, hc, j, :], XA[:, b * TB + (hc * CT + j), :], mv[:, hc, j, 0:1],
                                                 rs2[:, hc, j:j + 1], ALU.subtract, ALU.mult)
                    last.then_inc(s_xb, 1)
                for hc in range(HC):
                    dve.wait_ge(s_lp, b * HC + hc + 1)
                    dve.tensor_tensor(LG[:, :, bass.ds(b * TB + hc * CT, CT)].rearrange("p e t -> p t e"),
                                      PS[:, 2 * hc, 0:CT * E].rearrange("p (t e) -> p t e", t=CT),
                                      bsr[:, :].unsqueeze(1).broadcast_to([P, CT, E]), ALU.add).then_inc(s_lg, 1)
            dve.drain()
            logit_te = LG[:, :, :].rearrange("p e t -> p t e")
            dve.tensor_reduce(mx[:, :], logit_te, AX_X, ALU.max)
            dve.drain()
            dve.tensor_tensor(LG[:, :, :], LG[:, :, :], mx[:, :].unsqueeze(1).broadcast_to([P, E, NT]),
                              ALU.subtract).then_inc(s_sub, 1)
            dve.memset(base[:, :], 0)
            dve.wait_ge(s_pe, 1)
            dve.tensor_reduce(sm[:, :], logit_te, AX_X, ALU.add)
            dve.drain()
            dve.reciprocal(rsm[:, :], sm[:, :])
            dve.drain()
            dve.tensor_tensor(LG[:, :, :], LG[:, :, :], rsm[:, :].unsqueeze(1).broadcast_to([P, E, NT]),
                              ALU.mult).then_inc(s_pr, 1)
            with dve.Fori(0, ROUNDS // 2) as it:
                for i in range(2):
                    r = it * 2 + i
                    dve.tensor_tensor(thr[:, :, :], jbits[:, r, :].unsqueeze(2).broadcast_to([P, NTHR + 1, E]),
                                      base[:, :].unsqueeze(1).broadcast_to([P, NTHR + 1, E]),
                                      ALU.bitwise_or).then_inc(s_th, 1)
                    dve.wait_ge(s_th, it * 6 + (3 * i + 1))
                    dve.tensor_tensor(reach[:, :, :, :],
                                      LG[:, :, :].rearrange("p e t -> p t e").unsqueeze(2).broadcast_to([P, NT, NTHR, E]),
                                      thr[:, 1:, :].bitcast(F32).unsqueeze(1).broadcast_to([P, NT, NTHR, E]),
                                      ALU.is_ge).then_inc(s_cn, 1)
                    dve.wait_ge(s_ct, r + 1)
                    dve.scalar_tensor_tensor(thr[:, 1:, :].bitcast(F32),
                                             PS[:, 7, 0:NTHR * E].rearrange("p (j e) -> p j e", e=E), KSEL - 0.5,
                                             thr[:, 1:, :].bitcast(F32), ALU.is_ge, ALU.mult).then_inc(s_th, 1)
                    dve.wait_ge(s_th, it * 6 + (3 * i + 2))
                    dve.tensor_reduce(base[:, :].bitcast(F32), thr[:, :, :].bitcast(F32).rearrange("p j e -> p e j"), AX_X,
                                      ALU.max).then_inc(s_th, 1)
                    dve.wait_ge(s_th, it * 6 + (3 * i + 3))
            kth = base[:, :].bitcast(F32).unsqueeze(2).broadcast_to([P, E, NT])
            dve.tensor_tensor(ge[:, 0, :, :], LG[:, :, :], kth, ALU.is_gt)
            dve.tensor_tensor(ge[:, 1, :, :], LG[:, :, :], kth, ALU.is_equal).then_inc(s_rw, 1)
            flat = lambda a: a.rearrange("p e t -> p (e t)")

            def ranks(tile_totals, among_tile):
                dve.tensor_copy(tot[:, :, :], tile_totals)
                dve.drain()
                dve.tensor_tensor_scan(flat(run[:, :, :]), flat(fresh[:, :, :]), flat(tot[:, :, :]), 0.0, ALU.mult, ALU.add)
                dve.drain()
                dve.tensor_tensor(rank[:, :, :], run[:, :, :], tot[:, :, :], ALU.subtract)
                dve.drain()
                dve.tensor_tensor(rank[:, :, :], rank[:, :, :], among_tile, ALU.add)
                dve.drain()

            et = lambda a: a.rearrange("p (e t) -> p e t", e=E)
            dve.wait_ge(s_rt, 1)
            ranks(et(PS[:, 6, P:2 * P]), et(PS[:, 6, 2 * P:3 * P]))
            dve.tensor_reduce(need[:, :], et(PS[:, 6, 0:P]), AX_X, ALU.add)
            dve.drain()
            dve.tensor_scalar(need[:, :], need[:, :], -1.0, float(KSEL), ALU.mult, ALU.add)
            dve.drain()
            dve.tensor_tensor(rank[:, :, :], rank[:, :, :], need[:, :].unsqueeze(2).broadcast_to([P, E, NT]), ALU.is_lt)
            dve.drain()
            dve.tensor_tensor(rank[:, :, :], rank[:, :, :], ge[:, 1, :, :], ALU.mult)
            dve.drain()
            dve.tensor_tensor(sel[:, :, :], rank[:, :, :], ge[:, 0, :, :], ALU.add).then_inc(s_rw, 1)
            dve.wait_ge(s_rt, 2)
            ranks(et(PS[:, 5, 0:P]), et(PS[:, 5, P:2 * P]))
            dve.scalar_tensor_tensor(rank[:, :, :], rank[:, :, :], 1.0, sel[:, :, :], ALU.add, ALU.mult)
            dve.drain()
            dve.tensor_scalar(slot[:, :, :], rank[:, :, :], -1.0, None, ALU.add)
            dve.drain()
            dve.tensor_scalar(shi[:, :, :], slot[:, :, :], 4, None, ALU.arith_shift_right)
            dve.tensor_scalar(slo[:, :, :], slot[:, :, :], LO - 1, None, ALU.bitwise_and)
            dve.drain()
            dve.tensor_copy(hib[:, :, :], shi[:, :, :])
            dve.tensor_copy(lob[:, :, :], slo[:, :, :])
            dve.drain()
            for dst, part in ((ohl, lob), (ohh, hib)):
                dve.tensor_tensor(dst[:, :, :, :], iota_b[:, 0:LO].unsqueeze(1).unsqueeze(1).broadcast_to([P, NT, E, LO]),
                                  part[:, :, :].rearrange("p e t -> p t e").unsqueeze(3).broadcast_to([P, NT, E, LO]),
                                  ALU.is_equal)
            dve.drain()
            dve.tensor_scalar(ohv[:, :, 0, :, :].rearrange("p t e l -> p t (e l)"),
                              ohl[:, :, :, :].rearrange("p t e l -> p t (e l)"), iota_pf[:, :], None, ALU.mult)
            dve.tensor_tensor(ohv[:, :, 1, :, :].rearrange("p t e l -> p t (e l)"),
                              ohl[:, :, :, :].rearrange("p t e l -> p t (e l)"),
                              iota_b[:, 0:NT].unsqueeze(2).broadcast_to([P, NT, E * LO]), ALU.mult).then_inc(s_oh, 1)
            dve.wait_ge(s_dp, 1)
            dve.tensor_tensor(dm[:, :, :, :].rearrange("p v e l -> p v e l"),
                              PS[:, 4, 0:2 * E * LO].rearrange("p (v e l) -> p v e l", v=2, e=E),
                              of_expert[:, :].unsqueeze(1).unsqueeze(3).broadcast_to([P, 2, E, LO]), ALU.mult)
            dve.drain()
            dve.tensor_reduce(dv[:, :, :], dm[:, :, :, :].rearrange("p v e l -> p v l e"), AX_X, ALU.add)
            dve.drain()
            dve.scalar_tensor_tensor(tok[:, :], dv[:, 1, :], float(P), dv[:, 0, :], ALU.mult, ALU.add)
            dve.drain()
            dve.tensor_tensor(spread[:, :, :], tok[:, :].unsqueeze(1).broadcast_to([P, LOW_HI, LO]),
                              of_slot8[:, :].unsqueeze(2).broadcast_to([P, LOW_HI, LO]), ALU.mult).then_inc(s_spd, 1)
            dve.wait_ge(s_ixp, 1)
            dve.memset(idx[:, E:E + 2, :], 0)
            dve.tensor_copy(idx[:, 0:E, :].rearrange("p e j -> p (e j)"), PS[:, 3, 0:E * SH])
            dve.drain()
            for u in range(2):
                dve.tensor_copy(gidx[u][:, :], idx[:, u, :]).then_inc(s_gi, 1)
            with dve.Fori(0, E // 2) as it:
                e = it * 2
                for u in range(2):
                    dve.wait_ge(s_xtu, e + (u + 1))
                    dve.tensor_copy(prob[u][:, :], xi[u][:, :, bass.ds(e + (DM + u), 1)].rearrange("p j o -> p (j o)"))
                    dve.drain()
                    dve.tensor_copy(gidx[u][:, :], idx[:, e + (u + 2), :]).then_inc(s_gi, 1)
                for u in range(2):
                    dve.wait_ge(s_o2, e + (u + 3))
                    dve.wait_ge(s_sc, e * 32 + (u * 32 + CLEARED - 32))
                    for j in range(SH):
                        dve.tensor_tensor(ost[u][:, j, :], PS[:, u, j * DM:(j + 1) * DM], b2r[:, e + u, :], ALU.add)
                    dve.tensor_copy(sidx[u][:, :], idx[:, e + u, :])
                    dve.drain()
                    for j in range(SH):
                        last = dve.tensor_scalar(ost[u][:, j, :], ost[u][:, j, :], prob[u][:, j:j + 1],
                                                 None, ALU.mult)
                    last.then_inc(s_os, 1)
            for c in range(NC5):
                dve.wait_ge(s_fl[c], 16)
                for j in range(CT):
                    dve.bn_stats(bst5[:, c, j, :], fin[:, c, j, :])
                dve.drain()
                for j in range(CT):
                    last = dve.bn_aggr(mv5[:, c, j, :], bst5[:, c, j, :])
                last.then_inc(s_st5, 1)
            for c in range(NC5):
                dve.wait_ge(s_r5, c + 1)
                dve.scalar_tensor_tensor(nb5[:, c, :], mv5[:, c, :, 0], -1.0, rs5[:, c, :], ALU.mult, ALU.mult).then_inc(s_nb, 1)
            for c in range(NC5):
                dve.wait_ge(s_nm, c + 1)
                dve.tensor_tensor(res[:, c, :, :], fin[:, c, :, :], XA[:, c * CT:(c + 1) * CT, :], ALU.add).then_inc(s_res, 1)

        @block.tensor
        def _(pe):
            pe.sem_inc(s_y, 2)
            pe.sem_inc(s_o2, 2)
            pe.wait_ge(s_id, 1)
            pe.wait_ge(s_w, 16 * NLOADS)
            pe.transpose(PS[:, 7, 0:NB1 + 6], vrows[:, :], ident[0:NB1 + 6, 0:NB1 + 6]).then_inc(s_vt, 1)
            with pe.Fori(0, B) as b:
                pe.wait_ge(s_lg, b * HC + 1)
                for hc in range(HC):
                    pe.wait_ge(s_xn, b * HC + hc + 1)
                    for j in range(CT):
                        last = pe.transpose(PS[:, hc, j * P:(j + 1) * P], xn[:, hc, j, :], ident[:, :])
                    last.then_inc(s_xtp, 1)
                for hc in range(HC):
                    pe.wait_ge(s_xt, b * HC + hc + 1)
                    for h in range(H):
                        last = pe.matmul(PS[:, 2 + 2 * hc + h, :], win[:, h * P:(h + 1) * P], xnT[:, hc, :],
                                         start=True, stop=True)
                    last.then_inc(s_xip, 1)
                pe.wait_ge(s_vc, 1)
                for hc in range(HC):
                    if hc == 1:
                        pe.wait_ge(s_xi, b * HC + 1)
                    for h in range(H):
                        last = pe.matmul(PS[:, ZB[hc] + h, :], win[:, DI + h * P:DI + (h + 1) * P], xnT[:, hc, :],
                                         start=True, stop=True)
                    last.then_inc(s_zp, 1)
                for hc in range(HC):
                    n = slice(hc * CH, (hc + 1) * CH)
                    pe.wait_ge(s_xc, b * HC + hc + 1)
                    for h in range(H):
                        last = pe.matmul(PS[0:XR, hc, :], xpw[:, h, :], XC[:, h, n], start=(h == 0), stop=(h == H - 1))
                    last.then_inc(s_dbp, 1)
                for hc in range(HC):
                    pe.wait_ge(s_db, b * HC + hc + 1)
                    pe.wait_ge(*((s_xi, b * HC + 2) if hc == 0 else (s_z, b * HC + 1)))
                    for h in range(H):
                        last = pe.matmul(PS[:, DTB[hc] + h, :], dtw[:, h * P:(h + 1) * P], dbl[0:R, hc, :],
                                         start=True, stop=True)
                    last.then_inc(s_dtp, 1)
                pe.wait_ge(s_dd, 1)
                pe.wait_ge(s_z, b * HC + 2)
                for h in range(H):
                    for hc in range(HC):
                        n = slice(hc * CH, (hc + 1) * CH)
                        pe.matmul(Y[:, h, n], diagd[:, h, :], XC[:, h, n], start=True, stop=False, skip_group_check=True)
                with pe.Fori(0, NS // RING) as it:
                    s = it * RING
                    for i in range(RING):
                        pe.wait_ge(s_g, b * NS + s + (i + 1 + RING))
                        for h in range(H):
                            for hc in range(HC):
                                n = slice(hc * CH, (hc + 1) * CH)
                                last = pe.matmul(Y[:, h, n], ident[:, :], G[:, i % 2, h, n], start=False, stop=False,
                                                 skip_group_check=True)
                        last.then_inc(s_y, 1)
                for hc in range(HC):
                    pe.wait_ge(s_yg, b * HC + hc + 1)
                    for j in range(CT):
                        t = slice((hc * CT + j) * P, (hc * CT + j + 1) * P)
                        for h in range(H):
                            last = pe.matmul(PS[:, 4 + 2 * hc, j * DM:(j + 1) * DM], SZ[:, h, t], outw[:, h, :],
                                             start=(h == 0), stop=(h == H - 1))
                    last.then_inc(s_op, 1)
                for hc in range(HC):
                    pe.wait_ge(s_hn, b * HC + hc + 1)
                    for j in range(CT):
                        last = pe.transpose(PS[:, 5 + 2 * hc, j * P:(j + 1) * P], hn[:, hc, j, :], ident[:, :])
                    last.then_inc(s_htp, 1)
                for hc in range(HC):
                    pe.wait_ge(s_ht, b * HC + hc + 1)
                    for f in range(FH):
                        last = pe.matmul(PS[:, 2 * hc + f, :], fcw[:, f * P:(f + 1) * P], hnT[:, hc, :],
                                         start=True, stop=True)
                    last.then_inc(s_fp, 1)
                for hc in range(HC):
                    pe.wait_ge(s_hd, b * HC + hc + 1)
                    for j in range(CT):
                        for f in range(FH):
                            last = pe.matmul(PS[:, 4 + 2 * hc, j * DM:(j + 1) * DM], rel[:, hc, f, j * P:(j + 1) * P],
                                             prw[:, f, :], start=(f == 0), stop=(f == FH - 1))
                    last.then_inc(s_pp, 1)
                for hc in range(HC):
                    pe.wait_ge(s_xb, b * HC + hc + 1)
                    for j in range(CT):
                        last = pe.transpose(PS[:, 5 + 2 * hc, j * P:(j + 1) * P], xb[:, hc, j, :], ident[:, :])
                    last.then_inc(s_xbp, 1)
                for hc in range(HC):
                    pe.wait_ge(s_xbt, b * HC + hc + 1)
                    for j in range(CT):
                        last = pe.matmul(PS[:, 2 * hc, j * E:(j + 1) * E], xbT[:, hc, j * P:(j + 1) * P], wsr[:, :],
                                         start=True, stop=True)
                    last.then_inc(s_lp, 1)
            pe.wait_ge(s_const, 2)
            with pe.Fori(0, ROUNDS) as r:
                pe.wait_ge(s_cn, r + 1)
                for t in range(NT):
                    last = pe.matmul(PS[:, 7, 0:NTHR * E], ones_b[:, :], reach[:, t, :, :].rearrange("p j e -> p (j e)"),
                                     start=(t == 0), stop=(t == NT - 1))
                last.then_inc(s_ct, 1)
            flat = lambda a: a.rearrange("p e t -> p (e t)")
            pe.wait_ge(s_rw, 1)
            for k in range(2):
                pe.matmul(PS[:, 6, k * P:(k + 1) * P], ones_b[:, :], flat(ge[:, k, :, :]), start=True, stop=True)
            pe.matmul(PS[:, 6, 2 * P:3 * P], earlier[:, :], flat(ge[:, 1, :, :]), start=True, stop=True).then_inc(s_rt, 1)
            pe.wait_ge(s_rw, 2)
            pe.matmul(PS[:, 5, 0:P], ones_b[:, :], flat(sel[:, :, :]), start=True, stop=True)
            pe.matmul(PS[:, 5, P:2 * P], earlier[:, :], flat(sel[:, :, :]), start=True, stop=True).then_inc(s_rt, 1)
            pe.wait_ge(s_oh, 1)
            for t in range(NT):
                last = pe.matmul(PS[:, 4, 0:2 * E * LO], ohh[:, t, :, :].rearrange("p e h -> p (e h)"),
                                 ohv[:, t, :, :, :].rearrange("p v e l -> p (v e l)"), start=(t == 0), stop=(t == NT - 1))
            last.then_inc(s_dp, 1)
            pe.wait_ge(s_spd, 1)
            pe.matmul(PS[:, 3, 0:E * SH], spread[:, :, :].rearrange("p a l -> p (a l)"),
                      of_half[:, :, :].rearrange("p e j -> p (e j)"), start=True, stop=True).then_inc(s_ixp, 1)
            with pe.Fori(0, E // 2) as it:
                e = it * 2
                for u in range(2):
                    pe.wait_ge(s_gt[u], e * 16 + 32)
                    pe.wait_ge(s_xit, e + (u + 1))
                    for j in range(SH):
                        last = pe.transpose(PS[:, 2 + u, j * P:(j + 1) * P], xi[u][:, j, 0:DM], ident[:, :])
                    last.then_inc(s_xtu, 1)
                for u in range(2):
                    pe.wait_ge(s_xit, e + (u + 3))
                    pe.wait_ge(s_wl[u], e * 16 + 32)
                    pe.wait_ge(s_ge, e + (u + 1))
                    for k in range(FK):
                        last = pe.matmul(PS[:, 4 + 2 * u + k // 2, (k % 2) * KSEL:(k % 2 + 1) * KSEL],
                                         w1s[:, u, k * P:(k + 1) * P], xiT[u][:, :], start=True, stop=True)
                    last.then_inc(s_hp, 1)
                for u in range(2):
                    pe.wait_ge(s_ge, e + (u + 3))
                    pe.wait_ge(s_os, e + (u + 1))
                    for j in range(SH):
                        o = PS[:, u, j * DM:(j + 1) * DM]
                        for k in range(FK):
                            last = pe.matmul(o, hT[u][:, k, j * P:(j + 1) * P], w2s[:, u, k, :],
                                             start=(k == 0), stop=(k == FK - 1))
                    last.then_inc(s_o2, 1)


_INS = ["x", "in_proj_w", "conv_w", "conv_b", "x_proj_w", "dt_proj_w", "dt_proj_b", "A_log", "D", "out_proj_w",
        "c_fc_w", "c_proj_w"]
_TURNED = {"in_proj_w", "x_proj_w", "dt_proj_w", "out_proj_w", "c_fc_w", "c_proj_w"}
_FFN = ["Ws", "bs", "W1", "b1", "W2", "b2"]


def kernel(**inputs):
    import numpy as _np
    import concourse.bacc as _bacc
    from concourse import mybir as _mybir
    from concourse.bass_utils import run_bass_kernel_spmd as _run

    nc = _bacc.Bacc("TRN2", target_bir_lowering=False, num_devices=1)
    arrays, args = {}, []
    for name in ["L0_attn_" + n for n in _INS] + ["L0_ffn_" + n for n in _FFN]:
        a = _np.asarray(inputs[name])
        if name.removeprefix("L0_attn_") in _TURNED:
            a = a.T
        a = _np.ascontiguousarray(a)
        arrays[f"in_{name}_dram"] = a
        args.append(nc.dram_tensor(f"in_{name}_dram", a.shape, _mybir.dt.from_np(a.dtype), kind="ExternalInput").ap())
    out = nc.dram_tensor("out_0_dram", inputs["L0_attn_x"].shape, _mybir.dt.float32, kind="ExternalOutput").ap()
    sandwich_kernel(nc, *args, out)
    r = _run(nc, [arrays], core_ids=[0])
    return r.results[0]["out_0_dram"]
```

```python
from contextlib import ExitStack

import concourse.bass as bass
from concourse import mybir

ALU = mybir.AluOpType
ACT = mybir.ActivationFunctionType
F32 = mybir.dt.float32
BF16 = mybir.dt.bfloat16
I32 = mybir.dt.int32
AX_X = mybir.AxisListType.X

LN_EPS = 1e-05
RMS_EPS = 2.0 ** -23
ONE_BITS = 30


def sandwich_kernel(nc, x, in_w_t, conv_w, conv_b, xp_w_t, dt_w_t, dt_b, a_log, d_skip, out_w_t,
                    fc_w_t, pr_w_t, ws, bs, w1, b1, w2, b2, out):
    B, T, DM = x.shape
    DI = conv_w.shape[0]
    NS = a_log.shape[1]
    TAPS = conv_w.shape[1]
    R = dt_w_t.shape[0]
    E, _, F = w1.shape
    P = 128
    N = B * T
    NT = N // P
    TB = T // P
    CH = 512
    HC = T // CH
    CT = CH // P
    H = DI // P
    XR = R + 2 * NS
    LO = 16
    KSEL = N // E
    SH = KSEL // P
    HI = KSEL // LO
    LOW_HI = P // LO
    FK = F // P
    FH = fc_w_t.shape[1] // P
    RING = 4
    STEP_BITS = 3
    NTHR = 2 ** STEP_BITS - 1
    ROUNDS = ONE_BITS // STEP_BITS
    CLEARED = 48
    NC = B * HC
    NLOADS = 14
    assert E * HI == P and DM == P and H == 2 and HC == 2 and TB == 8 and E * NT == P and SH == 2 and FH == 2 and 2 * NC == 8
    assert NS % RING == 0 and ROUNDS * STEP_BITS == ONE_BITS

    bc_dram = nc.dram_tensor("bc_rows", (B, 2, NS, T), F32, kind="Internal").ap()
    ROW = DM + E
    xb_dram = nc.dram_tensor("ffn_in_rows", (N, ROW), F32, kind="Internal").ap()
    fin_dram = nc.dram_tensor("ffn_sum_rows", (N, DM), F32, kind="Internal").ap()

    with ExitStack() as ctx:
        def sb(name, shape, dt=F32):
            return ctx.enter_context(nc.sbuf_tensor(name, shape, dt))

        def sem(name):
            return ctx.enter_context(nc.semaphore(name))

        win = sb("win", [P, 2 * DI])
        convw = sb("convw", [P, H, TAPS])
        xpw = sb("xpw", [P, H, XR])
        dtw = sb("dtw", [R, DI])
        outw = sb("outw", [P, H, DM])
        fcw = sb("fcw", [P, FH * P])
        prw = sb("prw", [P, FH, DM])
        wsr = sb("wsr", [P, E])
        bsr = sb("bsr", [P, E])
        b2r = sb("b2r", [P, E, DM])
        NB1 = E * FK
        vrows = sb("vrows", [NB1 + 6, P])
        vcol = sb("vcol", [P, NB1 + 6])
        alog = sb("alog", [P, H, NS])
        aexp = sb("aexp", [P, H, NS])
        aneg = sb("aneg", [P, H, NS])
        ident = sb("ident", [P, P])
        diagd = sb("diagd", [P, H, P])
        expn = sb("expn", [P, 2 * CT])
        ones_b = sb("ones_b", [P, P], BF16)
        earlier = sb("earlier_token", [P, P], BF16)
        iota_p = sb("iota_p", [P, 1], I32)
        iota_pf = sb("iota_pf", [P, 1])
        iota_n = sb("iota_n", [P, 2 * LO], I32)
        iota_b = sb("iota_b", [P, 2 * LO], BF16)
        grp = sb("grp", [P, 3], I32)
        grpf = sb("grpf", [P, 3])
        of_expert = sb("of_expert", [P, E])
        of_slot8 = sb("of_slot8", [P, LOW_HI])
        of_half = sb("of_half", [P, E, SH])
        fresh = sb("fresh", [P, E, NT])
        jrow = sb("jrow", [P, NTHR + 1], I32)
        jbits = sb("jbits", [P, ROUNDS, NTHR + 1], I32)
        zero = sb("zero", [P, P])

        X = sb("X", [P, NT, DM])
        XA = sb("XA", [P, NT, DM])
        LG = sb("LG", [P, E, NT])
        XC = sb("XC", [P, B, H, T])
        SZ = sb("SZ", [P, B, H, T])
        DT = sb("DT", [P, B, H, T])
        DU = sb("DU", [P, B, H, T])
        DA = sb("DA", [P, 2, H, T])
        DB = sb("DB", [P, RING, H, T])
        BC = sb("BC", [P, RING, 2, T])
        bst = sb("bst", [P, NC, CT, 6])
        mv = sb("mv", [P, NC, CT, 2])
        vv = sb("vv", [P, NC, 2, CT])
        rs = sb("rs", [P, NC, 2, CT])
        DAf = DA[:, :, :, :].rearrange("p r h t -> p (r h t)")
        DBf = DB[:, :, :, :].rearrange("p r h t -> p (r h t)")
        BCf = BC[:, :, :, :].rearrange("p r w t -> p (r w t)")

        def lent(ring, at, *dims):
            n = 1
            for d in dims:
                n *= d
            names = " ".join(f"d{i}" for i in range(len(dims)))
            kw = {f"d{i}": d for i, d in enumerate(dims)}
            v = ring[:, at:at + n]
            return v.rearrange(f"p ({names}) -> p {names}", **kw) if len(dims) > 1 else v

        NX = H * (TAPS - 1 + T)
        xin = lent(BCf, 0, B, H, TAPS - 1 + T)
        xn = lent(BCf, B * NX, NC, CT, DM)
        xnT = lent(DAf, 0, NC, CH)
        dbl = lent(DAf, NC * CH, NC, CH)
        tmp1 = [lent(DBf, (2 * b) * H * T, HC, H, CH) for b in range(B)]
        tmp2 = [lent(DBf, (2 * b + 1) * H * T, HC, H, CH) for b in range(B)]
        x2 = lent(DBf, 0, NC, CT, DM)
        hn = lent(DBf, 2048, NC, CT, DM)
        hnT = lent(DBf, 4096, NC, CH)
        xbT = lent(DBf, 6144, NC, CH)
        rel = lent(BCf, 0, NC, FH, CH)
        xb = lent(BCf, 4096, NC, CT, DM)
        sq = lent(BCf, 6144, NC, CT, DM)
        ssq = sb("ssq", [P, NC, CT])
        vv2 = sb("vv2", [P, NC, CT])
        rs2 = sb("rs2", [P, NC, CT])
        mx = sb("mx", [P, NT])
        sm = sb("sm", [P, NT])
        rsm = sb("rsm", [P, NT])
        PT = sb("PT", [P, NT, E])
        base = sb("base", [P, E], I32)
        thr = sb("thr", [P, NTHR + 1, E], I32)
        ge = sb("ge", [P, 2, E, NT], BF16)
        sel = sb("sel", [P, E, NT], BF16)
        tot = sb("tot", [P, E, NT])
        run = sb("run", [P, E, NT])
        need = sb("need", [P, E])
        rank = sb("rank", [P, E, NT])
        slot = sb("slot", [P, E, NT], I32)
        shi = sb("slot_high_i", [P, E, NT], I32)
        slo = sb("slot_low_i", [P, E, NT], I32)
        hib = sb("slot_high", [P, E, NT], BF16)
        lob = sb("slot_low", [P, E, NT], BF16)
        BCb = BCf.bitcast(BF16)
        ohh = lent(BCb, 0, NT, E, HI)
        ohl = lent(BCb, NT * E * HI, NT, E, LO)
        ohv = lent(BCb, NT * E * (HI + LO), NT, 2, E, LO)
        reach = lent(DAf.bitcast(BF16), 0, NT, NTHR, E)
        dm = sb("dm", [P, 2, E, LO])
        dv = sb("dv", [P, 2, LO])
        tok = sb("tok", [P, LO])
        spread = sb("spread", [P, LOW_HI, LO])
        idx = sb("idx", [P, E + 2, SH], I32)
        gidx = [sb(f"gidx{i}", [P, SH], I32) for i in range(2)]
        sidx = [sb(f"sidx{i}", [P, SH], I32) for i in range(2)]
        prob = [sb(f"prob{i}", [P, SH]) for i in range(2)]
        w1s = lent(DAf, 1024, 2, F)
        w2s = lent(DAf, 2048, 2, FK, DM)
        xi = [lent(DBf, i * 288, SH, ROW) for i in range(2)]
        xiT = [lent(DBf, 7168 + i * 256, KSEL) for i in range(2)]
        hT = [lent(DBf, 1024 + i * 1024, FK, KSEL) for i in range(2)]
        ost = [lent(DBf, 3072 + i * 256, SH, DM) for i in range(2)]
        NC5 = NT // CT
        bst5 = sb("bst5", [P, NC5, CT, 6])
        mv5 = sb("mv5", [P, NC5, CT, 2])
        vv5 = sb("vv5", [P, NC5, CT])
        rs5 = sb("rs5", [P, NC5, CT])
        nb5 = sb("nb5", [P, NC5, CT])
        fin = lent(DBf, 0, NT // CT, CT, DM)
        res = lent(DBf, 2048, NT // CT, CT, DM)

        PS = ctx.enter_context(nc.psum_tensor("PS", [P, 8, CH], F32))

        s_x = [sem(f"x_loaded{c}") for c in range(NC)]; s_wi = sem("in_weights_loaded"); s_w = sem("weights_loaded")
        s_const = sem("constants"); s_id = sem("identity_made"); s_vt = sem("vector_rows_turned"); s_vc = sem("vector_columns")
        s_ae = sem("a_exp"); s_an = sem("a_negated"); s_dd = sem("skip_diagonal")
        s_mv = sem("ln1_stats"); s_rs = sem("ln1_scales"); s_xn = sem("normed"); s_xtp = sem("normed_turned"); s_xt = sem("normed_t")
        s_xip = sem("x_in_product"); s_xi = sem("x_in"); s_zp = sem("z_product"); s_z = sem("gate_silu")
        s_cv = sem("convolved"); s_xc = sem("x_conv"); s_dbp = sem("x_dbl_product"); s_db = sem("x_dbl")
        s_bw = sem("bc_stored")
        s_dtp = sem("dt_product"); s_ex = sem("softplus_parts"); s_e1 = sem("softplus_head"); s_sp = sem("softplus_tail")
        s_du = sem("dt_u")
        s_bc = [sem(f"bc_slot_loaded{i}") for i in range(RING)]
        s_dA = sem("decay"); s_dB = sem("input_term"); s_h = sem("states"); s_g = sem("states_times_c"); s_y = sem("y_summed")
        s_yi = sem("y_started"); s_yg = sem("y_gated")
        s_op = sem("out_product"); s_x2 = sem("x2"); s_sq = sem("x2_squares"); s_r2 = sem("rms2_scales"); s_hn = sem("hn")
        s_htp = sem("hn_turned"); s_ht = sem("hn_t"); s_fp = sem("fc_product"); s_re = sem("relu"); s_hd = sem("relu_squared")
        s_pp = sem("proj_product"); s_st3 = sem("ln2_stats"); s_r3 = sem("ln2_scales"); s_st4 = sem("ln3_stats"); s_r4 = sem("ln3_scales")
        s_xb = sem("ffn_in"); s_xw = sem("ffn_in_stored")
        s_xbp = sem("ffn_in_turned"); s_xbt = sem("ffn_in_t"); s_lp = sem("logit_product"); s_lg = sem("logits")
        s_sub = sem("logits_less_max"); s_pe = sem("exp_logits"); s_pr = sem("probs")
        s_cn = sem("counts"); s_ct = sem("counts_summed"); s_rw = sem("row_sums"); s_rt = sem("rows_summed")
        s_gt = [sem(f"gathered{i}") for i in range(2)]
        s_wl = [sem(f"expert_weights{i}") for i in range(2)]
        s_xtu = sem("gathered_turned"); s_xit = sem("gathered_t"); s_hp = sem("w1_product"); s_ge = sem("gelu")
        s_o2 = sem("w2_product"); s_os = sem("expert_out"); s_sc = sem("scattered")
        s_fl = [sem(f"ffn_sum_loaded{i}") for i in range(NC5)]
        s_st5 = sem("ln4_stats"); s_r5 = sem("ln4_scales"); s_res = sem("result"); s_out = sem("stored"); s_pt = sem("probs_by_token"); s_pw = sem("probs_stored"); s_nm = sem("ln4_normed"); s_oh = sem("one_hots"); s_dp = sem("slot_tokens"); s_spd = sem("slot_tokens_spread"); s_ixp = sem("index_product"); s_nb = sem("ln4_shifts")
        s_past = sem("past_a_wait"); s_th = sem("thresholds"); s_gi = sem("gather_indices"); s_si = sem("scatter_indices"); s_v5 = sem("ln4_variances"); s_ab = sem("softplus_abs"); s_eu = sem("softplus_exp")

        convb = vcol[:, NB1:NB1 + 2]
        dtb = vcol[:, NB1 + 2:NB1 + 4]
        dcol = vcol[:, NB1 + 4:NB1 + 6]
        x_rows = x.rearrange("b (t p) d -> p (b t) d", p=P)
        out_rows = out.rearrange("b (t p) d -> p (b t) d", p=P)

        block = ctx.enter_context(nc.Block())

        @block.sync
        def _(sp):
            for c in range(NC):
                ts = slice(c * CT, (c + 1) * CT)
                sp.dma_start(X[:, ts, :], x_rows[:, ts, :]).then_inc(s_x[c], 16)
                if c == 0:
                    sp.dma_start(win[:, :], in_w_t).then_inc(s_wi, 16)
            loads = [
                (vrows[0:NB1, :], b1.rearrange("e (k p) -> (e k) p", p=P)),
                (vrows[NB1:NB1 + 2, :], conv_b.rearrange("(h p) -> h p", p=P)),
                (vrows[NB1 + 2:NB1 + 4, :], dt_b.rearrange("(h p) -> h p", p=P)),
                (vrows[NB1 + 4:NB1 + 6, :], d_skip.rearrange("(h p) -> h p", p=P)),
                (convw[:, :, :], conv_w.rearrange("(h p) k -> p h k", p=P)),
                (xpw[:, :, :], xp_w_t.rearrange("(h p) f -> p h f", p=P)),
                (dtw[:, :], dt_w_t), (alog[:, :, :], a_log.rearrange("(h p) s -> p h s", p=P)),
                (outw[:, :, :], out_w_t.rearrange("(h p) d -> p h d", p=P)),
                (fcw[:, :], fc_w_t), (prw[:, :, :], pr_w_t.rearrange("(h p) d -> p h d", p=P)),
                (wsr[:, :], ws), (bsr[:, :], bs.rearrange("(a e) -> a e", a=1).broadcast_to([P, E])),
                (b2r[:, :, :], b2.unsqueeze(0).broadcast_to([P, E, DM])),
            ]
            assert len(loads) == NLOADS
            for dst, src in loads:
                sp.dma_start(dst, src).then_inc(s_w, 16)
            for c in range(NC):
                b, hc = divmod(c, HC)
                sp.wait_ge(s_db, c + 1)
                sp.dma_start(bc_dram[b, :, :, hc * CH:(hc + 1) * CH].rearrange("w s n -> (w s) n"),
                             dbl[R:XR, c, :]).then_inc(s_bw, 16)
            sp.wait_ge(s_bw, 16 * NC)
            for b in range(B):
                with sp.Fori(0, NS // RING) as it:
                    s = it * RING
                    for i in range(RING):
                        sp.wait_ge(s_dB, s + (b * NS + i + 1))
                        sp.wait_ge(s_g, s + (b * NS + i + 1))
                        sp.dma_start(BC[:, i, :, :],
                                     bc_dram[b, :, s + i, :].unsqueeze(0).broadcast_to([P, 2, T])
                                     ).then_inc(s_bc[i], 16)
            for c in range(NC):
                sp.wait_ge(s_xb, c + 1)
                sp.dma_start(xb_dram.rearrange("(t p) d -> p t d", p=P)[:, c * CT:(c + 1) * CT, 0:DM],
                             xb[:, c, :, :]).then_inc(s_xw, 16)
            sp.wait_ge(s_pt, 1)
            sp.dma_start(xb_dram.rearrange("(t p) d -> p t d", p=P)[:, :, DM:ROW], PT[:, :, :]).then_inc(s_pw, 16)
            with sp.Fori(0, E // 2) as it:
                e = it * 2
                for u in range(2):
                    sp.wait_ge(s_o2, e + u + 1)
                    sp.dma_start(w1s[:, u, :], w1[e + u, :, :]).then_inc(s_wl[u], 16)
                    sp.dma_start(w2s[:, u, :, :], w2[e + u, :, :].rearrange("(k p) d -> p k d", p=P)
                                 ).then_inc(s_wl[u], 16)
            sp.wait_ge(s_sc, CLEARED + 32 * E)
            for c in range(NC5):
                sp.dma_start(fin[:, c, :, :], fin_dram.rearrange("(t p) d -> p t d", p=P)[:, c * CT:(c + 1) * CT, :]
                             ).then_inc(s_fl[c], 16)
            for c in range(NC5):
                sp.wait_ge(s_res, c + 1)
                sp.dma_start(out_rows[:, c * CT:(c + 1) * CT, :], res[:, c, :, :]).then_inc(s_out, 16)
            sp.wait_ge(s_out, 16 * NC5)

        @block.gpsimd
        def _(pool):
            pool.sem_inc(s_dB, RING)
            pool.memset(zero[:, :], 0.0)
            pool.memset(expn[:, :], -0.5)
            for b in range(B):
                pool.memset(xin[:, b, :, 0:TAPS - 1], 0.0)
            pool.memset(ident[:, :], 0.0)
            pool.memset(ones_b[:, :], 1.0)
            pool.memset(fresh[:, :, :], 1.0)
            pool.drain().then_inc(s_const, 1)
            pool.affine_select(out=ident[:, :], in_=ident[:, :], compare_op=ALU.not_equal, fill=1.0, base=0,
                               pattern=[[-1, P]], channel_multiplier=1).then_inc(s_id, 1)
            pool.affine_select(out=earlier[:, :], in_=ones_b[:, :], compare_op=ALU.is_ge, fill=0.0, base=-1,
                               pattern=[[1, P]], channel_multiplier=-1)
            pool.memset(fresh[:, :, 0:1], 0.0)
            pool.iota(iota_p[:, :], pattern=[[1, 1]], base=0, channel_multiplier=1)
            pool.iota(iota_n[:, :], pattern=[[1, 2 * LO]], base=0, channel_multiplier=0)
            pool.iota(jrow[:, :], pattern=[[1, NTHR + 1]], base=0, channel_multiplier=0)
            pool.drain().then_inc(s_const, 1)
            for c in range(NC):
                pool.wait_ge(s_mv, c + 1)
                pool.tensor_scalar(vv[:, c, 0, :], mv[:, c, :, 1], LN_EPS, None, ALU.add)
                pool.tensor_scalar(vv[:, c, 1, :], mv[:, c, :, 1], 1.0 + RMS_EPS, LN_EPS * RMS_EPS, ALU.mult, ALU.add)
                pool.drain()
                pool.tensor_tensor(rs[:, c, :, :].rearrange("p a t -> p (a t)"),
                                   vv[:, c, :, :].rearrange("p a t -> p (a t)"), expn[:, :],
                                   ALU.pow).then_inc(s_rs, 1)
            for t in range(0, NT, 6):
                n = min(6, NT - t)
                pool.dma_start(fin_dram.rearrange("(t p) d -> p t d", p=P)[:, t:t + n, :],
                               zero[:, :].unsqueeze(1).broadcast_to([P, n, DM])).then_inc(s_sc, 16)
            for c in range(NC):
                b, hc = divmod(c, HC)
                n = slice(hc * CH, (hc + 1) * CH)
                pool.wait_ge(s_e1, c + 1)
                pool.tensor_tensor(tmp1[b][:, hc, :, :], DU[:, b, :, n], tmp1[b][:, hc, :, :], ALU.subtract)
                pool.drain()
                pool.wait_ge(s_ex, c + 1)
                pool.tensor_tensor(tmp1[b][:, hc, :, :], tmp1[b][:, hc, :, :], tmp2[b][:, hc, :, :], ALU.add).then_inc(s_sp, 1)
            pool.wait_ge(s_du, HC)
            for b in range(B):
                with pool.Fori(0, NS // RING) as it:
                    s = it * RING
                    for i in range(RING):
                        if i == 2:
                            pool.wait_ge(s_du, NC)
                        pool.wait_ge(s_bc[i], s * (16 // RING) + (b * (NS // RING) * 16 + 16))
                        pool.wait_ge(s_y, s + (b * NS + i + 1))
                        pool.tensor_tensor(DB[:, i, :, :], DU[:, b, :, :],
                                           BC[:, i, 0, :].unsqueeze(1).broadcast_to([P, H, T]), ALU.mult
                                           ).then_inc(s_dB, 1)
            for c in range(NC):
                pool.wait_ge(s_sq, c + 1)
                pool.tensor_scalar(vv2[:, c, :], ssq[:, c, :], RMS_EPS, None, ALU.add)
                pool.drain()
                pool.tensor_tensor(rs2[:, c, :], vv2[:, c, :], expn[:, 0:CT], ALU.pow).then_inc(s_r2, 1)
            for stats, scales in ((s_st3, s_r3), (s_st4, s_r4)):
                for c in range(NC):
                    pool.wait_ge(stats, c + 1)
                    pool.tensor_scalar(vv2[:, c, :], mv[:, c, :, 1], LN_EPS, None, ALU.add)
                    pool.drain()
                    pool.tensor_tensor(rs2[:, c, :], vv2[:, c, :], expn[:, 0:CT], ALU.pow).then_inc(scales, 1)

            pool.wait_ge(s_pr, 1)
            pool.tensor_copy(PT[:, :, :], LG[:, :, :].rearrange("p e t -> p t e")).then_inc(s_pt, 1)

            def gather(u, n):
                pool.wait_ge(s_gi, n)
                pool.sem_inc(s_past, 1)
                for j in range(SH):
                    pool.indirect_dma_start(
                        out=xi[u][:, j, :], out_offset=None, in_=xb_dram[:, :],
                        in_offset=bass.IndirectOffsetOnAxis(ap=gidx[u][:, j:j + 1], axis=0)).then_inc(s_gt[u], 16)

            def scatter(e, u):
                pool.wait_ge(s_os, e + (u + 3))
                pool.wait_ge(s_sc, e * 32 + (u * 32 + CLEARED))
                pool.sem_inc(s_past, 1)
                for j in range(SH):
                    pool.indirect_dma_start(
                        out=fin_dram[:, :], out_offset=bass.IndirectOffsetOnAxis(ap=sidx[u][:, j:j + 1], axis=0),
                        in_=ost[u][:, j, :], in_offset=None, compute_op=ALU.add).then_inc(s_sc, 16)

            pool.wait_ge(s_xw, 16 * NC)
            pool.wait_ge(s_sc, CLEARED)
            pool.wait_ge(s_pw, 16)
            for u in range(2):
                gather(u, u + 1)
            with pool.Fori(0, E // 2 - 1) as it:
                e = it * 2
                for u in range(2):
                    gather(u, e + (u + 3))
                for u in range(2):
                    scatter(e, u)
            for u in range(2):
                scatter(E - 2, u)
            for c in range(NT // CT):
                pool.wait_ge(s_st5, c + 1)
                pool.tensor_scalar(vv5[:, c, :], mv5[:, c, :, 1], LN_EPS, None, ALU.add).then_inc(s_v5, 1)
                pool.wait_ge(s_v5, c + 1)
                pool.tensor_tensor(rs5[:, c, :], vv5[:, c, :], expn[:, 0:CT], ALU.pow).then_inc(s_r5, 1)

        @block.scalar
        def _(act):
            act.sem_inc(s_xit, 2)
            act.sem_inc(s_ge, 2)
            for c in range(NC):
                act.wait_ge(s_xtp, c + 1)
                act.copy(xnT[:, c, :], PS[:, 2 * c, :]).then_inc(s_xt, 1)
            for c in range(NC):
                b, hc = divmod(c, HC)
                act.wait_ge(s_xip, c + 1)
                act.copy(xin[:, b, :, TAPS - 1 + hc * CH:TAPS - 1 + (hc + 1) * CH],
                         PS[:, 2 * c:2 * c + 2, :]).then_inc(s_xi, 1)
            act.wait_ge(s_vc, 1)
            for c in range(NC):
                b, hc = divmod(c, HC)
                n = slice(hc * CH, (hc + 1) * CH)
                act.wait_ge(s_zp, c + 1)
                act.activation(SZ[:, b, :, n], PS[:, 2 * c:2 * c + 2, :], ACT.Silu).then_inc(s_z, 1)
            for c in range(NC):
                b, hc = divmod(c, HC)
                n = slice(hc * CH, (hc + 1) * CH)
                act.wait_ge(s_cv, c + 1)
                for h in range(H):
                    last = act.activation(XC[:, b, h, n], tmp2[b][:, hc, h, :], ACT.Silu, bias=convb[:, h:h + 1])
                last.then_inc(s_xc, 1)
            for c in range(NC):
                act.wait_ge(s_dbp, c + 1)
                act.copy(dbl[0:XR, c, :], PS[0:XR, 2 * c, :]).then_inc(s_db, 1)
            for c in range(NC):
                b, hc = divmod(c, HC)
                n = slice(hc * CH, (hc + 1) * CH)
                act.wait_ge(s_dtp, c + 1)
                for h in range(H):
                    act.activation(tmp2[b][:, hc, h, :], PS[:, 2 * c + h, :], ACT.Abs, bias=dtb[:, h:h + 1])
                    last = act.activation(DT[:, b, h, n], PS[:, 2 * c + h, :], ACT.Relu, bias=dtb[:, h:h + 1])
                last.then_inc(s_ab, 1)
            act.activation(aexp[:, :, :], alog[:, :, :], ACT.Exp).then_inc(s_ae, 1)
            for c in range(NC):
                b, hc = divmod(c, HC)
                n = slice(hc * CH, (hc + 1) * CH)
                act.wait_ge(s_ab, c + 1)
                act.activation(DU[:, b, :, n], tmp2[b][:, hc, :, :], ACT.Exp, scale=-1.0).then_inc(s_eu, 1)
            for c in range(NC):
                b, hc = divmod(c, HC)
                n = slice(hc * CH, (hc + 1) * CH)
                act.wait_ge(s_eu, c + 1)
                act.activation(tmp2[b][:, hc, :, :], DU[:, b, :, n], ACT.Ln, bias=1.0).then_inc(s_ex, 1)
            act.wait_ge(s_an, 1)
            act.wait_ge(s_bw, 16 * NC)
            act.wait_ge(s_du, HC)
            for b in range(B):
                with act.Fori(0, NS // RING) as it:
                    s = it * RING
                    for i in range(RING):
                        act.wait_ge(s_h, s + (b * NS + i + 1))
                        for h in range(H):
                            last = act.activation(DA[:, i % 2, h, :], DT[:, b, h, :], ACT.Exp,
                                                  scale=aneg[:, h, bass.ds(s + i, 1)])
                        last.then_inc(s_dA, 1)
            for c in range(NC):
                act.wait_ge(s_x2, c + 1)
                for j in range(CT):
                    last = act.activation(sq[:, c, j, :], x2[:, c, j, :], ACT.Square, scale=float(DM) ** -0.5,
                                          accum_out=ssq[:, c, j:j + 1])
                last.then_inc(s_sq, 1)
            for c in range(NC):
                act.wait_ge(s_htp, c + 1)
                act.copy(hnT[:, c, :], PS[:, 2 * c + 1, :]).then_inc(s_ht, 1)
            for c in range(NC):
                act.wait_ge(s_fp, c + 1)
                act.activation(rel[:, c, :, :], PS[:, 2 * c:2 * c + 2, :], ACT.Relu).then_inc(s_re, 1)
            for c in range(NC):
                act.wait_ge(s_xbp, c + 1)
                act.copy(xbT[:, c, :], PS[:, 2 * c + 1, :]).then_inc(s_xbt, 1)
            act.wait_ge(s_sub, 1)
            act.activation(LG[:, :, :], LG[:, :, :], ACT.Exp).then_inc(s_pe, 1)
            with act.Fori(0, E // 2) as it:
                e = it * 2
                for u in range(2):
                    act.wait_ge(s_xtu, e + (u + 1))
                    act.copy(xiT[u][:, :], PS[:, 2 + u, 0:KSEL]).then_inc(s_xit, 1)
                for u in range(2):
                    act.wait_ge(s_hp, e + (u + 1))
                    act.wait_ge(s_o2, e + (u + 1))
                    for k in range(FK):
                        last = act.activation(hT[u][:, k, :], PS[:, 4 + 2 * u + k // 2, (k % 2) * KSEL:(k % 2 + 1) * KSEL],
                                              ACT.Gelu_apprx_tanh, bias=vcol[:, bass.ds(e * FK + (u * FK + k), 1)])
                    last.then_inc(s_ge, 1)
            for c in range(NC5):
                act.wait_ge(s_nb, c + 1)
                act.wait_ge(s_r5, c + 1)
                for j in range(CT):
                    last = act.activation(fin[:, c, j, :], fin[:, c, j, :], ACT.Identity, scale=rs5[:, c, j:j + 1],
                                          bias=nb5[:, c, j:j + 1])
                last.then_inc(s_nm, 1)

        @block.vector
        def _(dve):
            dve.sem_inc(s_g, RING)
            dve.sem_inc(s_h, 2)
            dve.sem_inc(s_os, 2)
            dve.wait_ge(s_const, 2)
            dve.tensor_copy(iota_b[:, :], iota_n[:, :])
            dve.tensor_copy(iota_pf[:, :], iota_p[:, :])
            for col, shift, mask in ((0, 4, 127), (1, 0, LOW_HI - 1), (2, 3, 127)):
                dve.tensor_scalar(grp[:, col:col + 1], iota_p[:, :], shift, mask, ALU.logical_shift_right, ALU.bitwise_and)
            for r in range(ROUNDS):
                dve.tensor_scalar(jbits[:, r, :], jrow[:, :], ONE_BITS - STEP_BITS * (r + 1), None, ALU.logical_shift_left)
            dve.drain()
            dve.tensor_copy(grpf[:, :], grp[:, :])
            dve.drain()
            for dst, n, col in ((of_expert[:, :], E, 0), (of_slot8[:, :], LOW_HI, 1),
                                (of_half[:, :, :].rearrange("p e j -> p (e j)"), E * SH, 2)):
                dve.tensor_scalar(dst, iota_n[:, 0:n], grpf[:, col:col + 1], None, ALU.is_equal)

            def layer_stats(rows, c, done):
                for j in range(CT):
                    dve.bn_stats(bst[:, c, j, :], rows(j))
                dve.drain()
                for j in range(CT):
                    last = dve.bn_aggr(mv[:, c, j, :], bst[:, c, j, :])
                last.then_inc(done, 1)

            for c in range(NC):
                dve.wait_ge(s_x[c], 16)
                layer_stats(lambda j: X[:, c * CT + j, :], c, s_mv)
            for c in range(NC):
                dve.wait_ge(s_rs, c + 1)
                for j in range(CT):
                    last = dve.tensor_scalar(xn[:, c, j, :], X[:, c * CT + j, :], mv[:, c, j, 0:1],
                                             rs[:, c, 1, j:j + 1], ALU.subtract, ALU.mult)
                last.then_inc(s_xn, 1)
            for t in range(NT):
                c, j = divmod(t, CT)
                dve.tensor_scalar(XA[:, t, :], X[:, t, :], mv[:, c, j, 0:1], rs[:, c, 0, j:j + 1], ALU.subtract, ALU.mult)
            dve.wait_ge(s_vt, 1)
            dve.tensor_copy(vcol[:, :], PS[:, 7, 0:NB1 + 6]).then_inc(s_vc, 1)
            dve.wait_ge(s_vc, 1)
            for h in range(H):
                last = dve.tensor_scalar(diagd[:, h, :], ident[:, :], dcol[:, h:h + 1], None, ALU.mult)
            last.then_inc(s_dd, 1)
            dve.wait_ge(s_w, 16 * NLOADS)
            for c in range(NC):
                b, hc = divmod(c, HC)
                dve.wait_ge(s_xi, c + 1)
                for k in range(TAPS):
                    for h in range(H):
                        shifted = xin[:, b, h, hc * CH + k:hc * CH + k + CH]
                        if k == 0:
                            last = dve.tensor_scalar(tmp2[b][:, hc, h, :], shifted, convw[:, h, 0:1], None, ALU.mult)
                        else:
                            last = dve.scalar_tensor_tensor(tmp2[b][:, hc, h, :], shifted, convw[:, h, k:k + 1],
                                                            tmp2[b][:, hc, h, :], ALU.mult, ALU.add)
                    if k < TAPS - 1:
                        dve.drain()
                last.then_inc(s_cv, 1)
            dve.wait_ge(s_ae, 1)
            dve.tensor_scalar(aneg[:, :, :], aexp[:, :, :], -1.0, None, ALU.mult).then_inc(s_an, 1)
            for c in range(NC):
                b, hc = divmod(c, HC)
                n = slice(hc * CH, (hc + 1) * CH)
                dve.wait_ge(s_eu, c + 1)
                dve.tensor_scalar(tmp1[b][:, hc, :, :], DU[:, b, :, n], 1.0, -1.0, ALU.add, ALU.add).then_inc(s_e1, 1)
            for c in range(NC):
                b, hc = divmod(c, HC)
                n = slice(hc * CH, (hc + 1) * CH)
                dve.wait_ge(s_sp, c + 1)
                dve.tensor_tensor(tmp1[b][:, hc, :, :], tmp1[b][:, hc, :, :], DU[:, b, :, n], ALU.min)
                dve.drain()
                dve.tensor_tensor(DT[:, b, :, n], DT[:, b, :, n], tmp1[b][:, hc, :, :], ALU.add)
                dve.drain()
                dve.tensor_tensor(DU[:, b, :, n], DT[:, b, :, n], XC[:, b, :, n], ALU.mult).then_inc(s_du, 1)
            for b in range(B):
                with dve.Fori(0, NS // RING) as it:
                    s = it * RING
                    for i in range(RING):
                        dve.wait_ge(s_dA, s + (b * NS + i + 1))
                        dve.wait_ge(s_dB, s + (b * NS + i + 1 + RING))
                        for h in range(H):
                            last = dve.tensor_tensor_scan(DB[:, i, h, :], DA[:, i % 2, h, :], DB[:, i, h, :], 0.0,
                                                          ALU.mult, ALU.add)
                        last.then_inc(s_h, 1)
                        dve.wait_ge(s_h, s + (b * NS + i + 3))
                        dve.tensor_tensor(DB[:, i, :, :], DB[:, i, :, :],
                                          BC[:, i, 1, :].unsqueeze(1).broadcast_to([P, H, T]), ALU.mult
                                          ).then_inc(s_g, 1)
            for c in range(NC):
                b, hc = divmod(c, HC)
                n = slice(hc * CH, (hc + 1) * CH)
                dve.wait_ge(s_y, (b + 1) * NS + RING)
                dve.tensor_tensor(SZ[:, b, :, n], PS[:, 2 * c:2 * c + 2, :], SZ[:, b, :, n], ALU.mult).then_inc(s_yg, 1)
            for c in range(NC):
                ts = slice(c * CT, (c + 1) * CT)
                dve.wait_ge(s_op, c + 1)
                dve.tensor_tensor(x2[:, c, :, :], XA[:, ts, :],
                                  PS[:, 2 * c, :].rearrange("p (t d) -> p t d", t=CT), ALU.add).then_inc(s_x2, 1)
            for c in range(NC):
                dve.wait_ge(s_r2, c + 1)
                for j in range(CT):
                    last = dve.tensor_scalar(hn[:, c, j, :], x2[:, c, j, :], rs2[:, c, j:j + 1], None, ALU.mult)
                last.then_inc(s_hn, 1)
            for c in range(NC):
                dve.wait_ge(s_re, c + 1)
                dve.tensor_tensor(rel[:, c, :, :], PS[:, 2 * c:2 * c + 2, :], rel[:, c, :, :], ALU.mult).then_inc(s_hd, 1)
            for c in range(NC):
                dve.wait_ge(s_pp, c + 1)
                dve.tensor_tensor(x2[:, c, :, :], x2[:, c, :, :],
                                  PS[:, 2 * c, :].rearrange("p (t d) -> p t d", t=CT), ALU.add)
                dve.drain()
                layer_stats(lambda j: x2[:, c, j, :], c, s_st3)
            for c in range(NC):
                ts = slice(c * CT, (c + 1) * CT)
                dve.wait_ge(s_r3, c + 1)
                for j in range(CT):
                    dve.tensor_scalar(x2[:, c, j, :], x2[:, c, j, :], mv[:, c, j, 0:1], rs2[:, c, j:j + 1],
                                      ALU.subtract, ALU.mult)
                dve.drain()
                dve.tensor_tensor(XA[:, ts, :], x2[:, c, :, :], X[:, ts, :], ALU.add)
                dve.drain()
                layer_stats(lambda j: XA[:, c * CT + j, :], c, s_st4)
            for c in range(NC):
                dve.wait_ge(s_r4, c + 1)
                for j in range(CT):
                    last = dve.tensor_scalar(xb[:, c, j, :], XA[:, c * CT + j, :], mv[:, c, j, 0:1],
                                             rs2[:, c, j:j + 1], ALU.subtract, ALU.mult)
                last.then_inc(s_xb, 1)
            for c in range(NC):
                dve.wait_ge(s_lp, c + 1)
                dve.tensor_tensor(LG[:, :, c * CT:(c + 1) * CT].rearrange("p e t -> p t e"),
                                  PS[:, 2 * c, 0:CT * E].rearrange("p (t e) -> p t e", t=CT),
                                  bsr[:, :].unsqueeze(1).broadcast_to([P, CT, E]), ALU.add)
            dve.drain()
            logit_te = LG[:, :, :].rearrange("p e t -> p t e")
            dve.tensor_reduce(mx[:, :], logit_te, AX_X, ALU.max)
            dve.drain()
            dve.tensor_tensor(LG[:, :, :], LG[:, :, :], mx[:, :].unsqueeze(1).broadcast_to([P, E, NT]),
                              ALU.subtract).then_inc(s_sub, 1)
            dve.memset(base[:, :], 0)
            dve.wait_ge(s_pe, 1)
            dve.tensor_reduce(sm[:, :], logit_te, AX_X, ALU.add)
            dve.drain()
            dve.reciprocal(rsm[:, :], sm[:, :])
            dve.drain()
            dve.tensor_tensor(LG[:, :, :], LG[:, :, :], rsm[:, :].unsqueeze(1).broadcast_to([P, E, NT]),
                              ALU.mult).then_inc(s_pr, 1)
            with dve.Fori(0, ROUNDS // 2) as it:
                for i in range(2):
                    r = it * 2 + i
                    dve.tensor_tensor(thr[:, :, :], jbits[:, r, :].unsqueeze(2).broadcast_to([P, NTHR + 1, E]),
                                      base[:, :].unsqueeze(1).broadcast_to([P, NTHR + 1, E]),
                                      ALU.bitwise_or).then_inc(s_th, 1)
                    dve.wait_ge(s_th, it * 6 + (3 * i + 1))
                    dve.tensor_tensor(reach[:, :, :, :],
                                      LG[:, :, :].rearrange("p e t -> p t e").unsqueeze(2).broadcast_to([P, NT, NTHR, E]),
                                      thr[:, 1:, :].bitcast(F32).unsqueeze(1).broadcast_to([P, NT, NTHR, E]),
                                      ALU.is_ge).then_inc(s_cn, 1)
                    dve.wait_ge(s_ct, r + 1)
                    dve.scalar_tensor_tensor(thr[:, 1:, :].bitcast(F32),
                                             PS[:, 7, 0:NTHR * E].rearrange("p (j e) -> p j e", e=E), KSEL - 0.5,
                                             thr[:, 1:, :].bitcast(F32), ALU.is_ge, ALU.mult).then_inc(s_th, 1)
                    dve.wait_ge(s_th, it * 6 + (3 * i + 2))
                    dve.tensor_reduce(base[:, :].bitcast(F32), thr[:, :, :].bitcast(F32).rearrange("p j e -> p e j"), AX_X,
                                      ALU.max).then_inc(s_th, 1)
                    dve.wait_ge(s_th, it * 6 + (3 * i + 3))
            kth = base[:, :].bitcast(F32).unsqueeze(2).broadcast_to([P, E, NT])
            dve.tensor_tensor(ge[:, 0, :, :], LG[:, :, :], kth, ALU.is_gt)
            dve.tensor_tensor(ge[:, 1, :, :], LG[:, :, :], kth, ALU.is_equal).then_inc(s_rw, 1)
            flat = lambda a: a.rearrange("p e t -> p (e t)")

            def ranks(tile_totals, among_tile):
                dve.tensor_copy(tot[:, :, :], tile_totals)
                dve.drain()
                dve.tensor_tensor_scan(flat(run[:, :, :]), flat(fresh[:, :, :]), flat(tot[:, :, :]), 0.0, ALU.mult, ALU.add)
                dve.drain()
                dve.tensor_tensor(rank[:, :, :], run[:, :, :], tot[:, :, :], ALU.subtract)
                dve.drain()
                dve.tensor_tensor(rank[:, :, :], rank[:, :, :], among_tile, ALU.add)
                dve.drain()

            et = lambda a: a.rearrange("p (e t) -> p e t", e=E)
            dve.wait_ge(s_rt, 1)
            ranks(et(PS[:, 6, P:2 * P]), et(PS[:, 6, 2 * P:3 * P]))
            dve.tensor_reduce(need[:, :], et(PS[:, 6, 0:P]), AX_X, ALU.add)
            dve.drain()
            dve.tensor_scalar(need[:, :], need[:, :], -1.0, float(KSEL), ALU.mult, ALU.add)
            dve.drain()
            dve.tensor_tensor(rank[:, :, :], rank[:, :, :], need[:, :].unsqueeze(2).broadcast_to([P, E, NT]), ALU.is_lt)
            dve.drain()
            dve.tensor_tensor(rank[:, :, :], rank[:, :, :], ge[:, 1, :, :], ALU.mult)
            dve.drain()
            dve.tensor_tensor(sel[:, :, :], rank[:, :, :], ge[:, 0, :, :], ALU.add).then_inc(s_rw, 1)
            dve.wait_ge(s_rt, 2)
            ranks(et(PS[:, 5, 0:P]), et(PS[:, 5, P:2 * P]))
            dve.scalar_tensor_tensor(rank[:, :, :], rank[:, :, :], 1.0, sel[:, :, :], ALU.add, ALU.mult)
            dve.drain()
            dve.tensor_scalar(slot[:, :, :], rank[:, :, :], -1.0, None, ALU.add)
            dve.drain()
            dve.tensor_scalar(shi[:, :, :], slot[:, :, :], 4, None, ALU.arith_shift_right)
            dve.tensor_scalar(slo[:, :, :], slot[:, :, :], LO - 1, None, ALU.bitwise_and)
            dve.drain()
            dve.tensor_copy(hib[:, :, :], shi[:, :, :])
            dve.tensor_copy(lob[:, :, :], slo[:, :, :])
            dve.drain()
            for dst, part in ((ohl, lob), (ohh, hib)):
                dve.tensor_tensor(dst[:, :, :, :], iota_b[:, 0:LO].unsqueeze(1).unsqueeze(1).broadcast_to([P, NT, E, LO]),
                                  part[:, :, :].rearrange("p e t -> p t e").unsqueeze(3).broadcast_to([P, NT, E, LO]),
                                  ALU.is_equal)
            dve.drain()
            dve.tensor_scalar(ohv[:, :, 0, :, :].rearrange("p t e l -> p t (e l)"),
                              ohl[:, :, :, :].rearrange("p t e l -> p t (e l)"), iota_pf[:, :], None, ALU.mult)
            dve.tensor_tensor(ohv[:, :, 1, :, :].rearrange("p t e l -> p t (e l)"),
                              ohl[:, :, :, :].rearrange("p t e l -> p t (e l)"),
                              iota_b[:, 0:NT].unsqueeze(2).broadcast_to([P, NT, E * LO]), ALU.mult).then_inc(s_oh, 1)
            dve.wait_ge(s_dp, 1)
            dve.tensor_tensor(dm[:, :, :, :].rearrange("p v e l -> p v e l"),
                              PS[:, 4, 0:2 * E * LO].rearrange("p (v e l) -> p v e l", v=2, e=E),
                              of_expert[:, :].unsqueeze(1).unsqueeze(3).broadcast_to([P, 2, E, LO]), ALU.mult)
            dve.drain()
            dve.tensor_reduce(dv[:, :, :], dm[:, :, :, :].rearrange("p v e l -> p v l e"), AX_X, ALU.add)
            dve.drain()
            dve.scalar_tensor_tensor(tok[:, :], dv[:, 1, :], float(P), dv[:, 0, :], ALU.mult, ALU.add)
            dve.drain()
            dve.tensor_tensor(spread[:, :, :], tok[:, :].unsqueeze(1).broadcast_to([P, LOW_HI, LO]),
                              of_slot8[:, :].unsqueeze(2).broadcast_to([P, LOW_HI, LO]), ALU.mult).then_inc(s_spd, 1)
            dve.wait_ge(s_ixp, 1)
            dve.memset(idx[:, E:E + 2, :], 0)
            dve.tensor_copy(idx[:, 0:E, :].rearrange("p e j -> p (e j)"), PS[:, 3, 0:E * SH])
            dve.drain()
            for u in range(2):
                dve.tensor_copy(gidx[u][:, :], idx[:, u, :]).then_inc(s_gi, 1)
            with dve.Fori(0, E // 2) as it:
                e = it * 2
                for u in range(2):
                    dve.wait_ge(s_xtu, e + (u + 1))
                    dve.tensor_copy(prob[u][:, :], xi[u][:, :, bass.ds(e + (DM + u), 1)].rearrange("p j o -> p (j o)"))
                    dve.drain()
                    dve.tensor_copy(gidx[u][:, :], idx[:, e + (u + 2), :]).then_inc(s_gi, 1)
                for u in range(2):
                    dve.wait_ge(s_o2, e + (u + 3))
                    dve.wait_ge(s_sc, e * 32 + (u * 32 + CLEARED - 32))
                    for j in range(SH):
                        dve.tensor_tensor(ost[u][:, j, :], PS[:, u, j * DM:(j + 1) * DM], b2r[:, e + u, :], ALU.add)
                    dve.tensor_copy(sidx[u][:, :], idx[:, e + u, :])
                    dve.drain()
                    for j in range(SH):
                        last = dve.tensor_scalar(ost[u][:, j, :], ost[u][:, j, :], prob[u][:, j:j + 1],
                                                 None, ALU.mult)
                    last.then_inc(s_os, 1)
            for c in range(NC5):
                dve.wait_ge(s_fl[c], 16)
                for j in range(CT):
                    dve.bn_stats(bst5[:, c, j, :], fin[:, c, j, :])
                dve.drain()
                for j in range(CT):
                    last = dve.bn_aggr(mv5[:, c, j, :], bst5[:, c, j, :])
                last.then_inc(s_st5, 1)
            for c in range(NC5):
                dve.wait_ge(s_r5, c + 1)
                dve.scalar_tensor_tensor(nb5[:, c, :], mv5[:, c, :, 0], -1.0, rs5[:, c, :], ALU.mult, ALU.mult).then_inc(s_nb, 1)
            for c in range(NC5):
                dve.wait_ge(s_nm, c + 1)
                dve.tensor_tensor(res[:, c, :, :], fin[:, c, :, :], XA[:, c * CT:(c + 1) * CT, :], ALU.add).then_inc(s_res, 1)

        @block.tensor
        def _(pe):
            pe.sem_inc(s_y, RING)
            pe.sem_inc(s_o2, 2)
            pe.wait_ge(s_id, 1)
            for c in range(NC):
                pe.wait_ge(s_xn, c + 1)
                for j in range(CT):
                    last = pe.transpose(PS[:, 2 * c, j * P:(j + 1) * P], xn[:, c, j, :], ident[:, :])
                last.then_inc(s_xtp, 1)
            pe.wait_ge(s_w, 16 * NLOADS)
            pe.transpose(PS[:, 7, 0:NB1 + 6], vrows[:, :], ident[0:NB1 + 6, 0:NB1 + 6]).then_inc(s_vt, 1)
            pe.wait_ge(s_wi, 16)
            for c in range(NC):
                pe.wait_ge(s_xt, c + 1)
                if c == NC - 1:
                    pe.wait_ge(s_vc, 1)
                for h in range(H):
                    last = pe.matmul(PS[:, 2 * c + h, :], win[:, h * P:(h + 1) * P], xnT[:, c, :],
                                     start=True, stop=True)
                last.then_inc(s_xip, 1)
            for c in range(NC):
                pe.wait_ge(s_xi, c + 1)
                for h in range(H):
                    last = pe.matmul(PS[:, 2 * c + h, :], win[:, DI + h * P:DI + (h + 1) * P], xnT[:, c, :],
                                     start=True, stop=True)
                last.then_inc(s_zp, 1)
            for c in range(NC):
                b, hc = divmod(c, HC)
                n = slice(hc * CH, (hc + 1) * CH)
                pe.wait_ge(s_xc, c + 1)
                for h in range(H):
                    last = pe.matmul(PS[0:XR, 2 * c, :], xpw[:, h, :], XC[:, b, h, n], start=(h == 0), stop=(h == H - 1))
                last.then_inc(s_dbp, 1)
            for c in range(NC):
                pe.wait_ge(s_db, c + 1)
                for h in range(H):
                    last = pe.matmul(PS[:, 2 * c + h, :], dtw[:, h * P:(h + 1) * P], dbl[0:R, c, :],
                                     start=True, stop=True)
                last.then_inc(s_dtp, 1)
            pe.wait_ge(s_dd, 1)
            for c in range(NC):
                b, hc = divmod(c, HC)
                pe.wait_ge(s_ab, c + 1)
                for h in range(H):
                    pe.matmul(PS[:, 2 * c + h, :], diagd[:, h, :], XC[:, b, h, hc * CH:(hc + 1) * CH],
                              start=True, stop=False, skip_group_check=True)
            for b in range(B):
                with pe.Fori(0, NS // RING) as it:
                    s = it * RING
                    for i in range(RING):
                        pe.wait_ge(s_g, s + (b * NS + i + 1 + RING))
                        for h in range(H):
                            for hc in range(HC):
                                last = pe.matmul(PS[:, 2 * (b * HC + hc) + h, :], ident[:, :],
                                                 DB[:, i, h, hc * CH:(hc + 1) * CH], start=False, stop=False,
                                                 skip_group_check=True)
                        last.then_inc(s_y, 1)
            for c in range(NC):
                b, hc = divmod(c, HC)
                pe.wait_ge(s_yg, c + 1)
                for j in range(CT):
                    t = slice((hc * CT + j) * P, (hc * CT + j + 1) * P)
                    for h in range(H):
                        last = pe.matmul(PS[:, 2 * c, j * DM:(j + 1) * DM], SZ[:, b, h, t], outw[:, h, :],
                                         start=(h == 0), stop=(h == H - 1))
                last.then_inc(s_op, 1)
            for c in range(NC):
                pe.wait_ge(s_hn, c + 1)
                for j in range(CT):
                    last = pe.transpose(PS[:, 2 * c + 1, j * P:(j + 1) * P], hn[:, c, j, :], ident[:, :])
                last.then_inc(s_htp, 1)
            for c in range(NC):
                pe.wait_ge(s_ht, c + 1)
                for f in range(FH):
                    last = pe.matmul(PS[:, 2 * c + f, :], fcw[:, f * P:(f + 1) * P], hnT[:, c, :],
                                     start=True, stop=True)
                last.then_inc(s_fp, 1)
            for c in range(NC):
                pe.wait_ge(s_hd, c + 1)
                for j in range(CT):
                    for f in range(FH):
                        last = pe.matmul(PS[:, 2 * c, j * DM:(j + 1) * DM], rel[:, c, f, j * P:(j + 1) * P],
                                         prw[:, f, :], start=(f == 0), stop=(f == FH - 1))
                last.then_inc(s_pp, 1)
            for c in range(NC):
                pe.wait_ge(s_xb, c + 1)
                for j in range(CT):
                    last = pe.transpose(PS[:, 2 * c + 1, j * P:(j + 1) * P], xb[:, c, j, :], ident[:, :])
                last.then_inc(s_xbp, 1)
            for c in range(NC):
                pe.wait_ge(s_xbt, c + 1)
                for j in range(CT):
                    last = pe.matmul(PS[:, 2 * c, j * E:(j + 1) * E], xbT[:, c, j * P:(j + 1) * P], wsr[:, :],
                                     start=True, stop=True)
                last.then_inc(s_lp, 1)
            pe.wait_ge(s_const, 2)
            with pe.Fori(0, ROUNDS) as r:
                pe.wait_ge(s_cn, r + 1)
                for t in range(NT):
                    last = pe.matmul(PS[:, 7, 0:NTHR * E], ones_b[:, :], reach[:, t, :, :].rearrange("p j e -> p (j e)"),
                                     start=(t == 0), stop=(t == NT - 1))
                last.then_inc(s_ct, 1)
            flat = lambda a: a.rearrange("p e t -> p (e t)")
            pe.wait_ge(s_rw, 1)
            for k in range(2):
                pe.matmul(PS[:, 6, k * P:(k + 1) * P], ones_b[:, :], flat(ge[:, k, :, :]), start=True, stop=True)
            pe.matmul(PS[:, 6, 2 * P:3 * P], earlier[:, :], flat(ge[:, 1, :, :]), start=True, stop=True).then_inc(s_rt, 1)
            pe.wait_ge(s_rw, 2)
            pe.matmul(PS[:, 5, 0:P], ones_b[:, :], flat(sel[:, :, :]), start=True, stop=True)
            pe.matmul(PS[:, 5, P:2 * P], earlier[:, :], flat(sel[:, :, :]), start=True, stop=True).then_inc(s_rt, 1)
            pe.wait_ge(s_oh, 1)
            for t in range(NT):
                last = pe.matmul(PS[:, 4, 0:2 * E * LO], ohh[:, t, :, :].rearrange("p e h -> p (e h)"),
                                 ohv[:, t, :, :, :].rearrange("p v e l -> p (v e l)"), start=(t == 0), stop=(t == NT - 1))
            last.then_inc(s_dp, 1)
            pe.wait_ge(s_spd, 1)
            pe.matmul(PS[:, 3, 0:E * SH], spread[:, :, :].rearrange("p a l -> p (a l)"),
                      of_half[:, :, :].rearrange("p e j -> p (e j)"), start=True, stop=True).then_inc(s_ixp, 1)
            with pe.Fori(0, E // 2) as it:
                e = it * 2
                for u in range(2):
                    pe.wait_ge(s_gt[u], e * 16 + 32)
                    pe.wait_ge(s_xit, e + (u + 1))
                    for j in range(SH):
                        last = pe.transpose(PS[:, 2 + u, j * P:(j + 1) * P], xi[u][:, j, 0:DM], ident[:, :])
                    last.then_inc(s_xtu, 1)
                for u in range(2):
                    pe.wait_ge(s_xit, e + (u + 3))
                    pe.wait_ge(s_wl[u], e * 16 + 32)
                    pe.wait_ge(s_ge, e + (u + 1))
                    for k in range(FK):
                        last = pe.matmul(PS[:, 4 + 2 * u + k // 2, (k % 2) * KSEL:(k % 2 + 1) * KSEL],
                                         w1s[:, u, k * P:(k + 1) * P], xiT[u][:, :], start=True, stop=True)
                    last.then_inc(s_hp, 1)
                for u in range(2):
                    pe.wait_ge(s_ge, e + (u + 3))
                    pe.wait_ge(s_os, e + (u + 1))
                    for j in range(SH):
                        o = PS[:, u, j * DM:(j + 1) * DM]
                        for k in range(FK):
                            last = pe.matmul(o, hT[u][:, k, j * P:(j + 1) * P], w2s[:, u, k, :],
                                             start=(k == 0), stop=(k == FK - 1))
                    last.then_inc(s_o2, 1)


_INS = ["x", "in_proj_w", "conv_w", "conv_b", "x_proj_w", "dt_proj_w", "dt_proj_b", "A_log", "D", "out_proj_w",
        "c_fc_w", "c_proj_w"]
_TURNED = {"in_proj_w", "x_proj_w", "dt_proj_w", "out_proj_w", "c_fc_w", "c_proj_w"}
_FFN = ["Ws", "bs", "W1", "b1", "W2", "b2"]


def kernel(**inputs):
    import numpy as _np
    import concourse.bacc as _bacc
    from concourse import mybir as _mybir
    from concourse.bass_utils import run_bass_kernel_spmd as _run

    nc = _bacc.Bacc("TRN2", target_bir_lowering=False, num_devices=1)
    arrays, args = {}, []
    for name in ["L0_attn_" + n for n in _INS] + ["L0_ffn_" + n for n in _FFN]:
        a = _np.asarray(inputs[name])
        if name.removeprefix("L0_attn_") in _TURNED:
            a = a.T
        a = _np.ascontiguousarray(a)
        arrays[f"in_{name}_dram"] = a
        args.append(nc.dram_tensor(f"in_{name}_dram", a.shape, _mybir.dt.from_np(a.dtype), kind="ExternalInput").ap())
    out = nc.dram_tensor("out_0_dram", inputs["L0_attn_x"].shape, _mybir.dt.float32, kind="ExternalOutput").ap()
    sandwich_kernel(nc, *args, out)
    r = _run(nc, [arrays], core_ids=[0])
    return r.results[0]["out_0_dram"]
```

```python
from contextlib import ExitStack

import concourse.bass as bass
from concourse import mybir

ALU = mybir.AluOpType
ACT = mybir.ActivationFunctionType
F32 = mybir.dt.float32
BF16 = mybir.dt.bfloat16
I32 = mybir.dt.int32
AX_X = mybir.AxisListType.X

LN_EPS = 1e-05
RMS_EPS = 2.0 ** -23
ONE_BITS = 30


def sandwich_kernel(nc, x, in_w_t, conv_w, conv_b, xp_w_t, dt_w_t, dt_b, a_log, d_skip, out_w_t,
                    fc_w_t, pr_w_t, ws, bs, w1, b1, w2, b2, out):
    B, T, DM = x.shape
    DI = conv_w.shape[0]
    NS = a_log.shape[1]
    TAPS = conv_w.shape[1]
    R = dt_w_t.shape[0]
    E, _, F = w1.shape
    P = 128
    N = B * T
    NT = N // P
    TB = T // P
    CH = 512
    HC = T // CH
    CT = CH // P
    H = DI // P
    XR = R + 2 * NS
    LO = 16
    KSEL = N // E
    SH = KSEL // P
    HI = KSEL // LO
    LOW_HI = P // LO
    FK = F // P
    FH = fc_w_t.shape[1] // P
    RING = 4
    XP = 4
    STEP_BITS = 3
    NTHR = 2 ** STEP_BITS - 1
    ROUNDS = ONE_BITS // STEP_BITS
    CLEARED = 48
    NC = B * HC
    AWAY = 256
    ROUNDS_UNROLLED = 5
    ACT5 = (0, 1, 3)
    DVE_DIFF = 2
    NLOADS = 13
    assert E * HI == P and DM == P and H == 2 and HC == 2 and TB == 8 and E * NT == P and SH == 2 and FH == 2 and 2 * NC == 8
    assert NS % RING == 0 and ROUNDS * STEP_BITS == ONE_BITS

    bc_dram = nc.dram_tensor("bc_rows", (B, 2, NS, T), F32, kind="Internal").ap()
    ROW = DM + E
    xb_dram = nc.dram_tensor("ffn_in_rows", (N, ROW), F32, kind="Internal").ap()
    fin_dram = nc.dram_tensor("ffn_sum_rows", (N, DM), F32, kind="Internal").ap()

    with ExitStack() as ctx:
        def sb(name, shape, dt=F32):
            return ctx.enter_context(nc.sbuf_tensor(name, shape, dt))

        def sem(name):
            return ctx.enter_context(nc.semaphore(name))

        win = sb("win", [P, 2 * DI])
        convw = sb("convw", [P, H, TAPS])
        xpw = sb("xpw", [P, H, XR])
        dtw = sb("dtw", [R, DI])
        outw = sb("outw", [P, H, DM])
        fcw = sb("fcw", [P, FH * P])
        prw = sb("prw", [P, FH, DM])
        wsr = sb("wsr", [P, E])
        bsr = sb("bsr", [P, E])
        b2r = sb("b2r", [P, E, DM])
        NB1 = E * FK
        vrows = sb("vrows", [NB1 + 6, P])
        vcol = sb("vcol", [P, NB1 + 6])
        alog = sb("alog", [P, H, NS])
        aexp = sb("aexp", [P, H, NS])
        aneg = sb("aneg", [P, H, NS])
        ident = sb("ident", [P, P])
        diagd = sb("diagd", [P, H, P])
        expn = sb("expn", [P, NT])
        ones_b = sb("ones_b", [P, P], BF16)
        earlier = sb("earlier_token", [P, P], BF16)
        iota_p = sb("iota_p", [P, 1], I32)
        iota_pf = sb("iota_pf", [P, 1])
        iota_n = sb("iota_n", [P, 2 * LO], I32)
        iota_b = sb("iota_b", [P, 2 * LO], BF16)
        grp = sb("grp", [P, 3], I32)
        grpf = sb("grpf", [P, 3])
        of_expert = sb("of_expert", [P, E])
        of_slot8 = sb("of_slot8", [P, LOW_HI])
        of_half = sb("of_half", [P, E, SH])
        fresh = sb("fresh", [P, 2, E, NT])
        jrow = sb("jrow", [P, NTHR + 1], I32)
        jbits = sb("jbits", [P, ROUNDS, NTHR + 1], I32)
        zero = sb("zero", [P, P])
        warm = sb("table_warmer", [P, 3])

        X = sb("X", [P, NT, DM])
        XA = sb("XA", [P, NT, DM])
        LG = sb("LG", [P, E, NT])
        XC = sb("XC", [P, B, H, T])
        SZ = sb("SZ", [P, B, H, T])
        DT = sb("DT", [P, B, H, T])
        DU = sb("DU", [P, B, H, T])
        DA = sb("DA", [P, 2, H, T])
        DB = sb("DB", [P, RING, H, T])
        BC = sb("BC", [P, RING, 2, T])
        bst = sb("bst", [P, NC, CT, 6])
        mv = sb("mv", [P, NC, CT, 2])
        vv = sb("vv", [P, NC, CT])
        rs = sb("rs", [P, NC, CT])
        vv1 = sb("vv1", [P, NC, CT])
        rs1 = sb("rs1", [P, NC, CT])
        nb1 = sb("nb1", [P, NC, CT])
        nm = sb("nm", [P, NC, CT])
        mv2 = sb("mv2", [P, 2, NC, CT, 2])
        rs3 = sb("rs3", [P, 2, NC, CT])
        nb3 = sb("nb3", [P, 2, NC, CT])
        DAf = DA[:, :, :, :].rearrange("p r h t -> p (r h t)")
        DBf = DB[:, :, :, :].rearrange("p r h t -> p (r h t)")
        BCf = BC[:, :, :, :].rearrange("p r w t -> p (r w t)")

        def lent(ring, at, *dims):
            n = 1
            for d in dims:
                n *= d
            names = " ".join(f"d{i}" for i in range(len(dims)))
            kw = {f"d{i}": d for i, d in enumerate(dims)}
            v = ring[:, at:at + n]
            return v.rearrange(f"p ({names}) -> p {names}", **kw) if len(dims) > 1 else v

        NX = H * (TAPS - 1 + T)
        xin = lent(BCf, 0, B, H, TAPS - 1 + T)
        xn = lent(BCf, B * NX, NC, CT, DM)
        xnT = lent(DAf, 0, NC, CH)
        dbl = lent(DAf, NC * CH, NC, CH)
        tmp1 = [lent(DBf, (2 * b) * H * T, HC, H, CH) for b in range(B)]
        tmp2 = [lent(DBf, (2 * b + 1) * H * T, HC, H, CH) for b in range(B)]
        ALL = NT * DM
        x2 = lent(BCf, 2 * ALL, NC, CT, DM)
        hn = lent(DBf, 1 * ALL, NC, CT, DM)
        hnT = lent(DBf, 2 * ALL, NC, CH)
        xbT = lent(DBf, 3 * ALL, NC, CH)
        rel = lent(BCf, 0, NC, FH, CH)
        xb = lent(DBf, 0, NC, CT, DM)
        sq = lent(BCf, 3 * ALL, NC, CT, DM)
        ssq = sb("ssq", [P, NC, CT])
        vv2 = sb("vv2", [P, NC, CT])
        rs2 = sb("rs2", [P, NC, CT])
        mx = sb("mx", [P, NT])
        sm = sb("sm", [P, NT])
        rsm = sb("rsm", [P, NT])
        PT = sb("PT", [P, NT, E])
        base = sb("base", [P, E], I32)
        thr = sb("thr", [P, NTHR + 1, E], I32)
        ge = sb("ge", [P, 2, E, NT], BF16)
        sel = sb("sel", [P, E, NT], BF16)
        tot = sb("tot", [P, 2, E, NT])
        run = sb("run", [P, 2, E, NT])
        need = sb("need", [P, E])
        rank = sb("rank", [P, 2, E, NT])
        slot = sb("slot", [P, E, NT], I32)
        shi = sb("slot_high_i", [P, E, NT], I32)
        slo = sb("slot_low_i", [P, E, NT], I32)
        hib = sb("slot_high", [P, E, NT], BF16)
        lob = sb("slot_low", [P, E, NT], BF16)
        BCb = BCf.bitcast(BF16)
        ohh = lent(BCb, 0, NT, E, HI)
        ohl = lent(BCb, NT * E * HI, NT, E, LO)
        ohv = lent(BCb, NT * E * (HI + LO), NT, 2, E, LO)
        reach = lent(BCb, 2 * 3 * ALL, NT, NTHR, E)
        dm = sb("dm", [P, 2, E, LO])
        dv = sb("dv", [P, 2, LO])
        tok = sb("tok", [P, LO])
        spread = sb("spread", [P, LOW_HI, LO])
        idx = sb("idx", [P, E, SH], I32)
        prob = [sb(f"prob{i}", [P, SH]) for i in range(XP)]
        w1s = lent(DAf, 0, XP, F)
        w2s = lent(DAf, XP * F, XP, FK, DM)
        XI = XP * SH * ROW
        xi = [lent(DBf, i * SH * ROW, SH, ROW) for i in range(XP)]
        hT = [lent(DBf, XI + i * FK * KSEL, FK, KSEL) for i in range(2)]
        ost = [lent(DBf, XI + 2 * FK * KSEL + i * SH * DM, SH, DM) for i in range(2)]
        xiT = [lent(DBf, XI + 2 * FK * KSEL + 2 * SH * DM + i * KSEL, KSEL) for i in range(2)]
        NC5 = NT // CT
        mv5 = sb("mv5", [P, NC5, CT, 2])
        vv5 = sb("vv5", [P, NC5, CT])
        rs5 = sb("rs5", [P, NC5, CT])
        nb5 = sb("nb5", [P, NC5, CT])
        fin = lent(DBf, 0, NC5, CT, DM)
        res = lent(DBf, ALL, NC5, CT, DM)

        PS = ctx.enter_context(nc.psum_tensor("PS", [P, 8, CH], F32))

        s_x_loaded = [sem(f"x_loaded{c}") for c in range(NC)]
        s_in_weights_loaded = sem("in_weights_loaded")
        s_weights_loaded = sem("weights_loaded")
        s_constants = sem("constants")
        s_identity_made = sem("identity_made")
        s_vector_rows_turned = sem("vector_rows_turned")
        s_vector_columns = sem("vector_columns")
        s_a_exp = sem("a_exp")
        s_a_negated = sem("a_negated")
        s_skip_diagonal = sem("skip_diagonal")
        s_ln1_stats = sem("ln1_stats")
        s_ln1_scales = sem("ln1_scales")
        s_normed = sem("normed")
        s_normed_turned = sem("normed_turned")
        s_normed_t = sem("normed_t")
        s_x_in_product = sem("x_in_product")
        s_x_in = sem("x_in")
        s_z_product = sem("z_product")
        s_gate_silu = sem("gate_silu")
        s_convolved = sem("convolved")
        s_x_conv = sem("x_conv")
        s_x_dbl_product = sem("x_dbl_product")
        s_x_dbl = sem("x_dbl")
        s_bc_stored = sem("bc_stored")
        s_dt_product = sem("dt_product")
        s_softplus_parts = sem("softplus_parts")
        s_softplus_head = sem("softplus_head")
        s_softplus_tail = sem("softplus_tail")
        s_dt_u = sem("dt_u")
        s_bc_slot_loaded = [sem(f"bc_slot_loaded{i}") for i in range(RING)]
        s_decay = sem("decay")
        s_input_term = sem("input_term")
        s_states = sem("states")
        s_states_times_c = sem("states_times_c")
        s_y_summed = sem("y_summed")
        s_y_gated = sem("y_gated")
        s_out_product = sem("out_product")
        s_x2 = sem("x2")
        s_x2_squares = sem("x2_squares")
        s_rms2_scales = sem("rms2_scales")
        s_hn = sem("hn")
        s_hn_turned = sem("hn_turned")
        s_hn_t = sem("hn_t")
        s_fc_product = sem("fc_product")
        s_relu = sem("relu")
        s_relu_squared = sem("relu_squared")
        s_proj_product = sem("proj_product")
        s_ln2_stats = sem("ln2_stats")
        s_ln2_scales = sem("ln2_scales")
        s_ln3_stats = sem("ln3_stats")
        s_ln3_scales = sem("ln3_scales")
        s_ffn_in = sem("ffn_in")
        s_ffn_in_stored = sem("ffn_in_stored")
        s_ffn_in_turned = sem("ffn_in_turned")
        s_ffn_in_t = sem("ffn_in_t")
        s_logit_product = sem("logit_product")
        s_logits_less_max = sem("logits_less_max")
        s_exp_logits = sem("exp_logits")
        s_probs = sem("probs")
        s_counts = sem("counts")
        s_counts_summed = sem("counts_summed")
        s_row_sums = sem("row_sums")
        s_rows_summed = sem("rows_summed")
        s_gathered = [sem(f"gathered{i}") for i in range(XP)]
        s_expert_weights = [sem(f"expert_weights{i}") for i in range(XP)]
        s_gathered_turned = sem("gathered_turned")
        s_gathered_t = sem("gathered_t")
        s_w1_product = sem("w1_product")
        s_gelu = sem("gelu")
        s_w2_product = sem("w2_product")
        s_expert_out = sem("expert_out")
        s_scattered = sem("scattered")
        s_ffn_sum_loaded = [sem(f"ffn_sum_loaded{i}") for i in range(NC5)]
        s_ln4_stats = sem("ln4_stats")
        s_ln4_scales = sem("ln4_scales")
        s_result = sem("result")
        s_stored = sem("stored")
        s_probs_by_token = sem("probs_by_token")
        s_probs_stored = sem("probs_stored")
        s_ln4_normed = sem("ln4_normed")
        s_one_hots = sem("one_hots")
        s_slot_tokens = sem("slot_tokens")
        s_slot_tokens_spread = sem("slot_tokens_spread")
        s_index_product = sem("index_product")
        s_ln4_shifts = sem("ln4_shifts")
        s_thresholds = sem("thresholds")
        s_indices = sem("indices")
        s_ln4_variances = sem("ln4_variances")
        s_softplus_abs = sem("softplus_abs")
        s_softplus_max = sem("softplus_max")
        s_conv_taps = sem("conv_taps")
        s_bn_stats = sem("bn_stats")
        s_tail_bounded = sem("tail_bounded")
        s_tail_added = sem("tail_added")
        s_states_first_half = sem("states_first_half")
        s_states_times_c_first_half = sem("states_times_c_first_half")
        s_ln2_normed_last_chunk = sem("ln2_normed_last_chunk")
        s_ffn_in_last_chunk = sem("ffn_in_last_chunk")
        s_tail_differences = sem("tail_differences")
        s_row_probs = sem("row_probs")
        s_ln1_shifts = sem("ln1_shifts")
        s_ln1 = sem("ln1")
        s_ln2_normed = sem("ln2_normed")
        s_softplus_exp = sem("softplus_exp")

        convb = vcol[:, NB1:NB1 + 2]
        dtb = vcol[:, NB1 + 2:NB1 + 4]
        dcol = vcol[:, NB1 + 4:NB1 + 6]
        x_rows = x.rearrange("b (t p) d -> p (b t) d", p=P)
        out_rows = out.rearrange("b (t p) d -> p (b t) d", p=P)

        block = ctx.enter_context(nc.Block())

        @block.sync
        def _(sp):
            for c in range(NC):
                ts = slice(c * CT, (c + 1) * CT)
                sp.dma_start(X[:, ts, :], x_rows[:, ts, :]).then_inc(s_x_loaded[c], 16)
                if c == 0:
                    sp.dma_start(win[:, :], in_w_t).then_inc(s_in_weights_loaded, 16)
                    sp.dma_start(convw[:, :, :], conv_w.rearrange("(h p) k -> p h k", p=P)).then_inc(s_in_weights_loaded, 16)
            loads = [
                (vrows[0:NB1, :], b1.rearrange("e (k p) -> (e k) p", p=P)),
                (vrows[NB1:NB1 + 2, :], conv_b.rearrange("(h p) -> h p", p=P)),
                (vrows[NB1 + 2:NB1 + 4, :], dt_b.rearrange("(h p) -> h p", p=P)),
                (vrows[NB1 + 4:NB1 + 6, :], d_skip.rearrange("(h p) -> h p", p=P)),
                (xpw[:, :, :], xp_w_t.rearrange("(h p) f -> p h f", p=P)),
                (dtw[:, :], dt_w_t), (alog[:, :, :], a_log.rearrange("(h p) s -> p h s", p=P)),
                (outw[:, :, :], out_w_t.rearrange("(h p) d -> p h d", p=P)),
                (fcw[:, :], fc_w_t), (prw[:, :, :], pr_w_t.rearrange("(h p) d -> p h d", p=P)),
                (wsr[:, :], ws), (bsr[:, :], bs.rearrange("(a e) -> a e", a=1).broadcast_to([P, E])),
                (b2r[:, :, :], b2.unsqueeze(0).broadcast_to([P, E, DM])),
            ]
            assert len(loads) == NLOADS
            for dst, src in loads:
                sp.dma_start(dst, src).then_inc(s_weights_loaded, 16)
            for c in range(NC):
                b, hc = divmod(c, HC)
                sp.wait_ge(s_x_dbl, c + 1)
                sp.dma_start(bc_dram[b, :, :, hc * CH:(hc + 1) * CH].rearrange("w s n -> (w s) n"),
                             dbl[R:XR, c, :]).then_inc(s_bc_stored, 16)
            sp.wait_ge(s_bc_stored, 16 * NC)
            for b in range(B):
                with sp.Fori(0, NS // RING) as it:
                    s = it * RING
                    for i in range(RING):
                        sp.wait_ge(s_input_term, s + (b * NS + i + 1))
                        sp.wait_ge(s_states_times_c, s + (b * NS + i + 1))
                        sp.dma_start(BC[:, i, :, :],
                                     bc_dram[b, :, s + i, :].unsqueeze(0).broadcast_to([P, 2, T])
                                     ).then_inc(s_bc_slot_loaded[i], 16)
            for c in range(NC):
                sp.wait_ge(*((s_ffn_in, c + 1) if c < NC - 1 else (s_ffn_in_last_chunk, 1)))
                sp.dma_start(xb_dram.rearrange("(t p) d -> p t d", p=P)[:, c * CT:(c + 1) * CT, 0:DM],
                             xb[:, c, :, :]).then_inc(s_ffn_in_stored, 16)
            def load_expert(e):
                sp.dma_start(w1s[:, e % XP, :], w1[e, :, :]).then_inc(s_expert_weights[e % XP], 16)
                sp.dma_start(w2s[:, e % XP, :, :], w2[e, :, :].rearrange("(k p) d -> p k d", p=P)
                             ).then_inc(s_expert_weights[e % XP], 16)

            for e in range(XP):
                load_expert(e)
            sp.wait_ge(s_probs_by_token, 1)
            sp.dma_start(xb_dram.rearrange("(t p) d -> p t d", p=P)[:, :, DM:ROW], PT[:, :, :]).then_inc(s_probs_stored, 16)
            for e in range(XP, E):
                sp.wait_ge(s_w2_product, 2 + e - XP + 1)
                load_expert(e)
            sp.wait_ge(s_scattered, CLEARED + 32 * E)
            for c in range(NC5):
                sp.dma_start(fin[:, c, :, :], fin_dram.rearrange("(t p) d -> p t d", p=P)[:, c * CT:(c + 1) * CT, :]
                             ).then_inc(s_ffn_sum_loaded[c], 16)
            for c in range(NC5):
                sp.wait_ge(s_result, c + 1)
                sp.dma_start(out_rows[:, c * CT:(c + 1) * CT, :], res[:, c, :, :]).then_inc(s_stored, 16)
            sp.wait_ge(s_stored, 16 * NC5)

        @block.gpsimd
        def _(pool):
            pool.sem_inc(s_input_term, RING)
            pool.memset(zero[:, :], 0.0)
            pool.memset(expn[:, :], -0.5)
            for b in range(B):
                pool.memset(xin[:, b, :, 0:TAPS - 1], 0.0)
            pool.memset(ident[:, :], 0.0)
            pool.memset(ones_b[:, :], 1.0)
            pool.memset(fresh[:, :, :, :], 1.0)
            pool.drain().then_inc(s_constants, 1)
            pool.affine_select(out=ident[:, :], in_=ident[:, :], compare_op=ALU.not_equal, fill=1.0, base=0,
                               pattern=[[-1, P]], channel_multiplier=1).then_inc(s_identity_made, 1)
            pool.affine_select(out=earlier[:, :], in_=ones_b[:, :], compare_op=ALU.is_ge, fill=0.0, base=-1,
                               pattern=[[1, P]], channel_multiplier=-1)
            pool.memset(fresh[:, :, :, 0:1], 0.0)
            pool.iota(iota_p[:, :], pattern=[[1, 1]], base=0, channel_multiplier=1)
            pool.iota(iota_n[:, :], pattern=[[1, 2 * LO]], base=0, channel_multiplier=0)
            pool.iota(jrow[:, :], pattern=[[1, NTHR + 1]], base=0, channel_multiplier=0)
            pool.drain().then_inc(s_constants, 1)
            for c in range(NC):
                pool.wait_ge(s_ln1_stats, c + 1)
                pool.tensor_scalar(vv[:, c, :], mv[:, c, :, 1], 1.0 + RMS_EPS, LN_EPS * RMS_EPS, ALU.mult, ALU.add)
                pool.drain()
                pool.tensor_tensor(rs[:, c, :], vv[:, c, :], expn[:, 0:CT], ALU.pow).then_inc(s_ln1_scales, 1)
            pool.tensor_scalar(vv1[:, :, :], mv[:, :, :, 1], LN_EPS, None, ALU.add)
            pool.tensor_scalar(nb1[:, :, :], mv[:, :, :, 0], -1.0, None, ALU.mult)
            pool.drain()
            pool.tensor_tensor(rs1[:, :, :].rearrange("p c t -> p (c t)"), vv1[:, :, :].rearrange("p c t -> p (c t)"),
                               expn[:, :], ALU.pow)
            pool.drain()
            pool.tensor_tensor(nb1[:, :, :], nb1[:, :, :], rs1[:, :, :], ALU.mult).then_inc(s_ln1_shifts, 1)
            for t in range(0, NT, 6):
                n = min(6, NT - t)
                pool.dma_start(fin_dram.rearrange("(t p) d -> p t d", p=P)[:, t:t + n, :],
                               zero[:, :].unsqueeze(1).broadcast_to([P, n, DM])).then_inc(s_scattered, 16)

            def tail_difference(c, nth):
                b, hc = divmod(c, HC)
                rest = tmp1[b][:, hc, :, :]
                pool.wait_ge(s_softplus_head, nth)
                pool.tensor_tensor(rest, DU[:, b, :, hc * CH:(hc + 1) * CH], rest, ALU.subtract)

            def tail_sum(c):
                b, hc = divmod(c, HC)
                rest = tmp1[b][:, hc, :, :]
                pool.wait_ge(s_softplus_parts, c + 1)
                if c == DVE_DIFF:
                    pool.wait_ge(s_tail_differences, 1)
                else:
                    pool.drain()
                pool.tensor_tensor(rest, rest, tmp2[b][:, hc, :, :], ALU.add).then_inc(s_softplus_tail, 1)

            tail_difference(0, 1)
            tail_difference(1, 2)
            tail_sum(0)
            tail_sum(1)
            tail_sum(2)
            tail_difference(3, 3)
            tail_sum(3)
            pool.wait_ge(s_dt_u, HC)
            for b in range(B):
                with pool.Fori(0, NS // RING) as it:
                    s = it * RING
                    for i in range(RING):
                        if i == 2:
                            pool.wait_ge(s_dt_u, NC)
                        pool.wait_ge(s_bc_slot_loaded[i], s * (16 // RING) + (b * (NS // RING) * 16 + 16))
                        pool.wait_ge(s_y_summed, s + (b * NS + i + 1))
                        pool.tensor_tensor(DB[:, i, :, :], DU[:, b, :, :],
                                           BC[:, i, 0, :].unsqueeze(1).broadcast_to([P, H, T]), ALU.mult
                                           ).then_inc(s_input_term, 1)
            for c in range(NC):
                pool.wait_ge(s_x2_squares, c + 1)
                pool.tensor_scalar(vv2[:, c, :], ssq[:, c, :], RMS_EPS, None, ALU.add)
                pool.drain()
                pool.tensor_tensor(rs2[:, c, :], vv2[:, c, :], expn[:, 0:CT], ALU.pow).then_inc(s_rms2_scales, 1)
            def scale_and_shift(k, c):
                pool.wait_ge((s_ln2_stats, s_ln3_stats)[k], c + 1)
                pool.tensor_scalar(vv2[:, c, :], mv2[:, k, c, :, 1], LN_EPS, None, ALU.add)
                pool.tensor_scalar(nm[:, c, :], mv2[:, k, c, :, 0], -1.0, None, ALU.mult)
                pool.drain()
                pool.tensor_tensor(rs3[:, k, c, :], vv2[:, c, :], expn[:, 0:CT], ALU.pow)
                pool.drain()
                pool.tensor_tensor(nb3[:, k, c, :], nm[:, c, :], rs3[:, k, c, :], ALU.mult).then_inc((s_ln2_scales, s_ln3_scales)[k], 1)

            scale_and_shift(0, 0)
            scale_and_shift(0, 1)
            scale_and_shift(1, 0)
            scale_and_shift(0, 2)
            scale_and_shift(1, 1)
            scale_and_shift(0, 3)
            scale_and_shift(1, 2)
            scale_and_shift(1, 3)

            pool.wait_ge(s_probs, 1)
            pool.tensor_copy(PT[:, :, :], LG[:, :, :].rearrange("p e t -> p t e")).then_inc(s_probs_by_token, 1)

            def gather(e):
                if e >= XP:
                    pool.wait_ge(s_row_probs, e - XP + 1)
                for j in range(SH):
                    pool.indirect_dma_start(
                        out=xi[e % XP][:, j, :], out_offset=None, in_=xb_dram[:, :],
                        in_offset=bass.IndirectOffsetOnAxis(ap=idx[:, e, j:j + 1], axis=0)).then_inc(s_gathered[e % XP], 16)

            def scatter(e):
                pool.wait_ge(s_expert_out, 2 + e + 1)
                pool.wait_ge(s_scattered, CLEARED + e * 32)
                for j in range(SH):
                    pool.indirect_dma_start(
                        out=fin_dram[:, :], out_offset=bass.IndirectOffsetOnAxis(ap=idx[:, e, j:j + 1], axis=0),
                        in_=ost[e % 2][:, j, :], in_offset=None, compute_op=ALU.add).then_inc(s_scattered, 16)

            pool.wait_ge(s_ffn_in_stored, 16 * NC)
            pool.wait_ge(s_scattered, CLEARED)
            pool.wait_ge(s_probs_stored, 16)
            pool.wait_ge(s_indices, 1)
            for e in range(E - 2):
                gather(e)
            scatter(0)
            gather(E - 2)
            scatter(1)
            gather(E - 1)
            for e in range(2, E):
                scatter(e)
            for c in range(NC5):
                pool.wait_ge(s_ln4_stats, c + 1)
                pool.tensor_scalar(vv5[:, c, :], mv5[:, c, :, 1], LN_EPS, None, ALU.add).then_inc(s_ln4_variances, 1)
                pool.wait_ge(s_ln4_variances, c + 1)
                pool.tensor_tensor(rs5[:, c, :], vv5[:, c, :], expn[:, 0:CT], ALU.pow).then_inc(s_ln4_scales, 1)

        @block.scalar
        def _(act):
            act.sem_inc(s_gathered_t, 2)
            act.sem_inc(s_gelu, 2)
            act.wait_ge(s_constants, 1)
            act.activation(warm[:, 0:1], zero[:, 0:1], ACT.Silu)
            def take_turned_x(c):
                act.wait_ge(s_normed_turned, c + 1)
                act.copy(xnT[:, c, :], PS[:, 2 * c, :]).then_inc(s_normed_t, 1)

            def take_x_in(c):
                b, hc = divmod(c, HC)
                act.wait_ge(s_x_in_product, c + 1)
                act.copy(xin[:, b, :, TAPS - 1 + hc * CH:TAPS - 1 + (hc + 1) * CH],
                         PS[:, 2 * c:2 * c + 2, :]).then_inc(s_x_in, 1)

            def silu_z(c):
                b, hc = divmod(c, HC)
                act.wait_ge(s_z_product, c + 1)
                act.activation(SZ[:, b, :, hc * CH:(hc + 1) * CH], PS[:, 2 * c:2 * c + 2, :], ACT.Silu).then_inc(s_gate_silu, 1)

            def silu_conv(c):
                b, hc = divmod(c, HC)
                act.wait_ge(s_convolved, c + 1)
                for h in range(H):
                    last = act.activation(XC[:, b, h, hc * CH:(hc + 1) * CH], tmp2[b][:, hc, h, :], ACT.Silu,
                                          bias=convb[:, h:h + 1])
                last.then_inc(s_x_conv, 1)

            def take_x_dbl(c):
                act.wait_ge(s_x_dbl_product, c + 1)
                act.copy(dbl[0:XR, c, :], PS[0:XR, 2 * c, :]).then_inc(s_x_dbl, 1)

            def absolute(c):
                b, hc = divmod(c, HC)
                act.wait_ge(s_dt_product, c + 1)
                for h in range(H):
                    last = act.activation(tmp2[b][:, hc, h, :], PS[:, 2 * c + h, :], ACT.Abs, bias=dtb[:, h:h + 1])
                last.then_inc(s_softplus_abs, 1)

            def exponential(c):
                b, hc = divmod(c, HC)
                act.wait_ge(s_softplus_abs, c + 1)
                act.activation(DU[:, b, :, hc * CH:(hc + 1) * CH], tmp2[b][:, hc, :, :], ACT.Exp, scale=-1.0
                               ).then_inc(s_softplus_exp, 1)

            def logarithm(c):
                b, hc = divmod(c, HC)
                act.wait_ge(s_softplus_exp, c + 1)
                act.activation(tmp2[b][:, hc, :, :], DU[:, b, :, hc * CH:(hc + 1) * CH], ACT.Ln, bias=1.0
                               ).then_inc(s_softplus_parts, 1)

            for c in range(2):
                take_turned_x(c)
                take_x_in(c)
            act.wait_ge(s_vector_rows_turned, 1)
            act.copy(vcol[:, :], PS[:, 7, 0:NB1 + 6]).then_inc(s_vector_columns, 1)
            act.wait_ge(s_vector_columns, 1)
            take_turned_x(2)
            silu_conv(0)
            take_x_in(2)
            take_x_dbl(0)
            take_turned_x(3)
            silu_conv(1)
            take_x_in(3)
            absolute(0)
            take_x_dbl(1)
            silu_conv(2)
            absolute(1)
            take_x_dbl(2)
            silu_conv(3)
            exponential(0)
            exponential(1)
            act.activation(aexp[:, :, :], alog[:, :, :], ACT.Exp).then_inc(s_a_exp, 1)
            absolute(2)
            take_x_dbl(3)
            exponential(2)
            logarithm(0)
            logarithm(1)
            absolute(3)
            logarithm(2)
            exponential(3)
            logarithm(3)
            for c in range(NC):
                silu_z(c)
            act.wait_ge(s_a_negated, 1)
            act.wait_ge(s_bc_stored, 16 * NC)
            act.wait_ge(s_dt_u, HC)
            for b in range(B):
                with act.Fori(0, NS // RING) as it:
                    s = it * RING
                    for i in range(RING):
                        act.wait_ge(s_states, s + (b * NS + i + 1))
                        for h in range(H):
                            last = act.activation(DA[:, i % 2, h, :], DT[:, b, h, :], ACT.Exp,
                                                  scale=aneg[:, h, bass.ds(s + i, 1)])
                        last.then_inc(s_decay, 1)
            act.wait_ge(s_ln1_shifts, 1)
            for t in range(NT):
                c, j = divmod(t, CT)
                last = act.activation(XA[:, t, :], X[:, t, :], ACT.Identity, scale=rs1[:, c, j:j + 1],
                                      bias=nb1[:, c, j:j + 1])
                if j == CT - 1:
                    last.then_inc(s_ln1, 1)

            def squares(c):
                act.wait_ge(s_x2, c + 1)
                for j in range(CT):
                    last = act.activation(sq[:, c, j, :], x2[:, c, j, :], ACT.Square, scale=float(DM) ** -0.5,
                                          accum_out=ssq[:, c, j:j + 1])
                last.then_inc(s_x2_squares, 1)

            def take_normed(c):
                act.wait_ge(s_hn_turned, c + 1)
                act.copy(hnT[:, c, :], PS[:, 2 * c + 1, :]).then_inc(s_hn_t, 1)

            def relu(c):
                act.wait_ge(s_fc_product, c + 1)
                act.activation(rel[:, c, :, :], PS[:, 2 * c:2 * c + 2, :], ACT.Relu).then_inc(s_relu, 1)

            def second_norm(c):
                act.wait_ge(s_ln2_scales, c + 1)
                for j in range(CT):
                    last = act.activation(x2[:, c, j, :], x2[:, c, j, :], ACT.Identity, scale=rs3[:, 0, c, j:j + 1],
                                          bias=nb3[:, 0, c, j:j + 1])
                last.then_inc(s_ln2_normed, 1)

            def third_norm(c):
                act.wait_ge(s_ln3_scales, c + 1)
                for j in range(CT):
                    last = act.activation(xb[:, c, j, :], XA[:, c * CT + j, :], ACT.Identity, scale=rs3[:, 1, c, j:j + 1],
                                          bias=nb3[:, 1, c, j:j + 1])
                last.then_inc(s_ffn_in, 1)

            def take_ffn_in(c):
                act.wait_ge(s_ffn_in_turned, c + 1)
                act.copy(xbT[:, c, :], PS[:, 2 * c + 1, :]).then_inc(s_ffn_in_t, 1)

            squares(0)
            squares(1)
            squares(2)
            take_normed(0)
            take_normed(1)
            squares(3)
            relu(0)
            take_normed(2)
            relu(1)
            take_normed(3)
            relu(2)
            second_norm(0)
            relu(3)
            second_norm(1)
            third_norm(0)
            second_norm(2)
            third_norm(1)
            take_ffn_in(0)
            third_norm(2)
            take_ffn_in(1)
            take_ffn_in(2)
            take_ffn_in(3)
            act.activation(warm[:, 1:2], zero[:, 0:1], ACT.Exp)
            act.wait_ge(s_logits_less_max, 1)
            act.activation(LG[:, :, :], LG[:, :, :], ACT.Exp).then_inc(s_exp_logits, 1)

            def take_turned(e):
                act.wait_ge(s_gathered_turned, e + 1)
                act.copy(xiT[e % 2][:, :], PS[:, 2 + e % 2, 0:KSEL]).then_inc(s_gathered_t, 1)

            def gelu(e):
                act.wait_ge(s_w1_product, e + 1)
                act.wait_ge(s_w2_product, e + 1)
                for k in range(FK):
                    last = act.activation(hT[e % 2][:, k, :],
                                          PS[:, 4 + 2 * (e % 2) + k // 2, (k % 2) * KSEL:(k % 2 + 1) * KSEL],
                                          ACT.Gelu_apprx_tanh, bias=vcol[:, e * FK + k:e * FK + k + 1])
                last.then_inc(s_gelu, 1)

            act.activation(warm[:, 2:3], zero[:, 0:1], ACT.Gelu_apprx_tanh)
            take_turned(0)
            for e in range(E):
                if (e + 1) % XP:
                    take_turned(e + 1)
                gelu(e)
                if (e + 1) % XP == 0 and e + 1 < E:
                    take_turned(e + 1)
            for k, c in enumerate(ACT5):
                act.wait_ge(s_ln4_shifts, k + 1)
                act.wait_ge(s_ln4_scales, c + 1)
                for j in range(CT):
                    last = act.activation(fin[:, c, j, :], fin[:, c, j, :], ACT.Identity, scale=rs5[:, c, j:j + 1],
                                          bias=nb5[:, c, j:j + 1])
                last.then_inc(s_ln4_normed, 1)

        @block.vector
        def _(dve):
            dve.sem_inc(s_states_times_c, RING)
            dve.sem_inc(s_states, 2)
            dve.sem_inc(s_expert_out, 2)
            stats_made = 0

            def layer_stats(rows, to, c, done):
                nonlocal stats_made
                for j in range(CT):
                    dve.bn_stats(bst[:, c, j, :], rows(j)).then_inc(s_bn_stats, 1)
                for j in range(CT):
                    stats_made += 1
                    dve.wait_ge(s_bn_stats, stats_made)
                    last = dve.bn_aggr(to[:, c, j, :], bst[:, c, j, :])
                last.then_inc(done, 1)

            def stats(c):
                dve.wait_ge(s_x_loaded[c], 16)
                layer_stats(lambda j: X[:, c * CT + j, :], mv, c, s_ln1_stats)

            def normed(c):
                dve.wait_ge(s_ln1_scales, c + 1)
                for j in range(CT):
                    last = dve.tensor_scalar(xn[:, c, j, :], X[:, c * CT + j, :], mv[:, c, j, 0:1],
                                             rs[:, c, j:j + 1], ALU.subtract, ALU.mult)
                last.then_inc(s_normed, 1)

            stats(0)
            for c in range(NC):
                if c + 1 < NC:
                    stats(c + 1)
                normed(c)
            def taps(c, k, h):
                return (c * (TAPS - 1) + k) * H + h + 1

            dve.wait_ge(s_in_weights_loaded, 32)
            for c in range(NC):
                b, hc = divmod(c, HC)
                if c == 1:
                    dve.wait_ge(s_vector_columns, 1)
                    for h in range(H):
                        last = dve.tensor_scalar(diagd[:, h, :], ident[:, :], dcol[:, h:h + 1], None, ALU.mult)
                    last.then_inc(s_skip_diagonal, 1)
                dve.wait_ge(s_x_in, c + 1)
                for k in range(TAPS):
                    for h in range(H):
                        shifted = xin[:, b, h, hc * CH + k:hc * CH + k + CH]
                        if k == 0:
                            last = dve.tensor_scalar(tmp2[b][:, hc, h, :], shifted, convw[:, h, 0:1], None, ALU.mult)
                        else:
                            dve.wait_ge(s_conv_taps, taps(c, k - 1, h))
                            last = dve.scalar_tensor_tensor(tmp2[b][:, hc, h, :], shifted, convw[:, h, k:k + 1],
                                                            tmp2[b][:, hc, h, :], ALU.mult, ALU.add)
                        if k < TAPS - 1:
                            last.then_inc(s_conv_taps, 1)
                last.then_inc(s_convolved, 1)
            def maximum(c):
                b, hc = divmod(c, HC)
                n = slice(hc * CH, (hc + 1) * CH)
                dve.wait_ge(s_softplus_abs, c + 1)
                for h in range(H):
                    last = dve.tensor_scalar(DT[:, b, h, n], PS[:, 2 * c + h, :], dtb[:, h:h + 1], 0.0, ALU.add, ALU.max)
                last.then_inc(s_softplus_max, 1)

            def log_argument(c):
                b, hc = divmod(c, HC)
                dve.wait_ge(s_softplus_exp, c + 1)
                last = dve.tensor_scalar(tmp1[b][:, hc, :, :], DU[:, b, :, hc * CH:(hc + 1) * CH], 1.0, -1.0,
                                         ALU.add, ALU.add)
                if c != DVE_DIFF:
                    last.then_inc(s_softplus_head, 1)

            def tail_difference(c):
                b, hc = divmod(c, HC)
                rest = tmp1[b][:, hc, :, :]
                dve.tensor_tensor(rest, DU[:, b, :, hc * CH:(hc + 1) * CH], rest, ALU.subtract).then_inc(s_tail_differences, 1)

            def tail(c):
                b, hc = divmod(c, HC)
                n = slice(hc * CH, (hc + 1) * CH)
                rest = tmp1[b][:, hc, :, :]
                dve.wait_ge(s_softplus_tail, c + 1)
                dve.tensor_tensor(rest, rest, DU[:, b, :, n], ALU.min)
                dve.drain()
                dve.tensor_tensor(DT[:, b, :, n], DT[:, b, :, n], rest, ALU.add)
                dve.drain()
                dve.tensor_tensor(DU[:, b, :, n], DT[:, b, :, n], XC[:, b, :, n], ALU.mult).then_inc(s_dt_u, 1)

            maximum(0)
            maximum(1)
            log_argument(0)
            log_argument(1)
            maximum(2)
            log_argument(2)
            dve.drain()
            tail_difference(2)
            dve.wait_ge(s_a_exp, 1)
            dve.tensor_scalar(aneg[:, :, :], aexp[:, :, :], -1.0, None, ALU.mult).then_inc(s_a_negated, 1)
            tail(0)
            maximum(3)
            log_argument(3)
            tail(1)
            b = 1
            part = [slice(hc * CH, (hc + 1) * CH) for hc in range(HC)]
            for hc, n in enumerate(part):
                dve.wait_ge(s_softplus_tail, HC + hc + 1)
                dve.tensor_tensor(tmp1[b][:, hc, :, :], tmp1[b][:, hc, :, :], DU[:, b, :, n], ALU.min).then_inc(s_tail_bounded, 1)
            for hc, n in enumerate(part):
                dve.wait_ge(s_tail_bounded, hc + 1)
                dve.tensor_tensor(DT[:, b, :, n], DT[:, b, :, n], tmp1[b][:, hc, :, :], ALU.add).then_inc(s_tail_added, 1)
            for hc, n in enumerate(part):
                dve.wait_ge(s_tail_added, hc + 1)
                dve.tensor_tensor(DU[:, b, :, n], DT[:, b, :, n], XC[:, b, :, n], ALU.mult).then_inc(s_dt_u, 1)

            def scan(b, s, i):
                dve.wait_ge(s_decay, s + (b * NS + i + 1))
                dve.wait_ge(s_input_term, s + (b * NS + i + 1 + RING))
                for h in range(H):
                    dve.tensor_tensor_scan(DB[:, i, h, :], DA[:, i % 2, h, :], DB[:, i, h, :], 0.0,
                                           ALU.mult, ALU.add).then_inc((s_states_first_half, s_states)[h], 1)

            def times_c(b, s, i):
                dve.wait_ge(s_states_first_half, s + (b * NS + i + 1))
                dve.tensor_tensor(DB[:, i, 0, :], DB[:, i, 0, :], BC[:, i, 1, :], ALU.mult).then_inc(s_states_times_c_first_half, 1)
                dve.wait_ge(s_states, s + (b * NS + i + 3))
                dve.tensor_tensor(DB[:, i, 1, :], DB[:, i, 1, :], BC[:, i, 1, :], ALU.mult).then_inc(s_states_times_c, 1)

            def scans(b, first, rings):
                with dve.Fori(0, rings) as it:
                    s = it * RING + first
                    for i in range(RING):
                        scan(b, s, i)
                        times_c(b, s, i)

            def gate(c):
                b, hc = divmod(c, HC)
                n = slice(hc * CH, (hc + 1) * CH)
                dve.wait_ge(s_y_summed, (b + 1) * NS + RING)
                dve.tensor_tensor(SZ[:, b, :, n], PS[:, 2 * c:2 * c + 2, :], SZ[:, b, :, n], ALU.mult).then_inc(s_y_gated, 1)

            def residual(c):
                dve.wait_ge(s_out_product, c + 1)
                dve.wait_ge(s_ln1, c + 1)
                dve.tensor_tensor(x2[:, c, :, :], XA[:, c * CT:(c + 1) * CT, :],
                                  PS[:, 2 * c, :].rearrange("p (t d) -> p t d", t=CT), ALU.add).then_inc(s_x2, 1)

            def rms_normed(c):
                dve.wait_ge(s_rms2_scales, c + 1)
                for j in range(CT):
                    last = dve.tensor_scalar(hn[:, c, j, :], x2[:, c, j, :], rs2[:, c, j:j + 1], None, ALU.mult)
                last.then_inc(s_hn, 1)

            scans(0, 0, NS // RING)
            scans(1, 0, 1)
            gate(0)
            gate(1)
            scans(1, RING, NS // RING - 1)

            def squared(c):
                dve.wait_ge(s_relu, c + 1)
                dve.tensor_tensor(rel[:, c, :, :], PS[:, 2 * c:2 * c + 2, :], rel[:, c, :, :], ALU.mult).then_inc(s_relu_squared, 1)

            def second_stats(c):
                dve.wait_ge(s_proj_product, c + 1)
                dve.tensor_tensor(x2[:, c, :, :], x2[:, c, :, :],
                                  PS[:, 2 * c, :].rearrange("p (t d) -> p t d", t=CT), ALU.add)
                dve.drain()
                layer_stats(lambda j: x2[:, c, j, :], mv2[:, 0], c, s_ln2_stats)

            def third_stats(c):
                ts = slice(c * CT, (c + 1) * CT)
                dve.wait_ge(*((s_ln2_normed, c + 1) if c < NC - 1 else (s_ln2_normed_last_chunk, 1)))
                dve.tensor_tensor(XA[:, ts, :], x2[:, c, :, :], X[:, ts, :], ALU.add)
                dve.drain()
                layer_stats(lambda j: XA[:, c * CT + j, :], mv2[:, 1], c, s_ln3_stats)

            residual(0)
            residual(1)
            dve.wait_ge(s_constants, 2)
            dve.tensor_copy(iota_b[:, :], iota_n[:, :])
            dve.tensor_copy(iota_pf[:, :], iota_p[:, :])
            for col, shift, mask in ((0, 4, 127), (1, 0, LOW_HI - 1), (2, 3, 127)):
                dve.tensor_scalar(grp[:, col:col + 1], iota_p[:, :], shift, mask, ALU.logical_shift_right, ALU.bitwise_and)
            for r in range(ROUNDS):
                dve.tensor_scalar(jbits[:, r, :], jrow[:, :], ONE_BITS - STEP_BITS * (r + 1), None, ALU.logical_shift_left)
            dve.drain()
            dve.tensor_copy(grpf[:, :], grp[:, :])
            dve.drain()
            for dst, n, col in ((of_expert[:, :], E, 0), (of_slot8[:, :], LOW_HI, 1),
                                (of_half[:, :, :].rearrange("p e j -> p (e j)"), E * SH, 2)):
                dve.tensor_scalar(dst, iota_n[:, 0:n], grpf[:, col:col + 1], None, ALU.is_equal)
            gate(2)
            gate(3)
            rms_normed(0)
            rms_normed(1)
            residual(2)
            residual(3)
            rms_normed(2)
            rms_normed(3)
            squared(0)
            squared(1)
            second_stats(0)
            squared(2)
            second_stats(1)
            squared(3)
            third_stats(0)
            second_stats(2)
            third_stats(1)
            second_stats(3)
            third_stats(2)
            c = NC - 1
            dve.wait_ge(s_ln2_scales, 4)
            for j in range(CT):
                last = dve.tensor_scalar(x2[:, c, j, :], x2[:, c, j, :], mv2[:, 0, c, j, 0:1], rs3[:, 0, c, j:j + 1],
                                         ALU.subtract, ALU.mult)
            last.then_inc(s_ln2_normed_last_chunk, 1)
            third_stats(c)
            dve.wait_ge(s_ln3_scales, 4)
            for j in range(CT):
                last = dve.tensor_scalar(xb[:, c, j, :], XA[:, c * CT + j, :], mv2[:, 1, c, j, 0:1],
                                         rs3[:, 1, c, j:j + 1], ALU.subtract, ALU.mult)
            last.then_inc(s_ffn_in_last_chunk, 1)
            for c in range(NC):
                dve.wait_ge(s_logit_product, c + 1)
                dve.tensor_tensor(LG[:, :, c * CT:(c + 1) * CT].rearrange("p e t -> p t e"),
                                  PS[:, 2 * c, 0:CT * E].rearrange("p (t e) -> p t e", t=CT),
                                  bsr[:, :].unsqueeze(1).broadcast_to([P, CT, E]), ALU.add)
            dve.drain()
            logit_te = LG[:, :, :].rearrange("p e t -> p t e")
            dve.tensor_reduce(mx[:, :], logit_te, AX_X, ALU.max)
            dve.drain()
            dve.tensor_tensor(LG[:, :, :], LG[:, :, :], mx[:, :].unsqueeze(1).broadcast_to([P, E, NT]),
                              ALU.subtract).then_inc(s_logits_less_max, 1)
            dve.memset(base[:, :], 0)
            dve.wait_ge(s_exp_logits, 1)
            dve.tensor_reduce(sm[:, :], logit_te, AX_X, ALU.add)
            dve.drain()
            dve.reciprocal(rsm[:, :], sm[:, :])
            dve.drain()
            dve.tensor_tensor(LG[:, :, :], LG[:, :, :], rsm[:, :].unsqueeze(1).broadcast_to([P, E, NT]),
                              ALU.mult).then_inc(s_probs, 1)
            with dve.Fori(0, ROUNDS // ROUNDS_UNROLLED) as it:
                for i in range(ROUNDS_UNROLLED):
                    r = it * ROUNDS_UNROLLED + i
                    dve.tensor_tensor(thr[:, :, :], jbits[:, r, :].unsqueeze(2).broadcast_to([P, NTHR + 1, E]),
                                      base[:, :].unsqueeze(1).broadcast_to([P, NTHR + 1, E]),
                                      ALU.bitwise_or).then_inc(s_thresholds, 1)
                    dve.wait_ge(s_thresholds, it * (3 * ROUNDS_UNROLLED) + (3 * i + 1))
                    for half in range(2):
                        ts = slice(half * NT // 2, (half + 1) * NT // 2)
                        dve.tensor_tensor(reach[:, ts, :, :],
                                          LG[:, :, ts].rearrange("p e t -> p t e").unsqueeze(2)
                                          .broadcast_to([P, NT // 2, NTHR, E]),
                                          thr[:, 1:, :].bitcast(F32).unsqueeze(1).broadcast_to([P, NT // 2, NTHR, E]),
                                          ALU.is_ge).then_inc(s_counts, 1)
                    dve.wait_ge(s_counts_summed, r + 1)
                    dve.scalar_tensor_tensor(thr[:, 1:, :].bitcast(F32),
                                             PS[:, 7, 0:NTHR * E].rearrange("p (j e) -> p j e", e=E), KSEL - 0.5,
                                             thr[:, 1:, :].bitcast(F32), ALU.is_ge, ALU.mult).then_inc(s_thresholds, 1)
                    dve.wait_ge(s_thresholds, it * (3 * ROUNDS_UNROLLED) + (3 * i + 2))
                    dve.tensor_reduce(base[:, :].bitcast(F32), thr[:, :, :].bitcast(F32).rearrange("p j e -> p e j"), AX_X,
                                      ALU.max).then_inc(s_thresholds, 1)
                    dve.wait_ge(s_thresholds, it * (3 * ROUNDS_UNROLLED) + (3 * i + 3))
            kth = base[:, :].bitcast(F32).unsqueeze(2).broadcast_to([P, E, NT])
            dve.tensor_tensor(ge[:, 0, :, :], LG[:, :, :], kth, ALU.is_gt)
            dve.tensor_tensor(ge[:, 1, :, :], LG[:, :, :], kth, ALU.is_equal).then_inc(s_row_sums, 1)
            dve.wait_ge(s_rows_summed, 1)
            by_kind = lambda a: a.rearrange("p (k e t) -> p k e t", k=2, e=E)
            row = lambda a: a.rearrange("p k e t -> p (k e t)")
            dve.tensor_copy(row(tot[:, :, :, :]), PS[:, 6, 0:2 * P])
            dve.drain()
            dve.tensor_tensor_scan(row(run[:, :, :, :]), row(fresh[:, :, :, :]), row(tot[:, :, :, :]), 0.0,
                                   ALU.mult, ALU.add)
            dve.tensor_reduce(need[:, :], tot[:, 0, :, :], AX_X, ALU.add)
            dve.drain()
            dve.tensor_tensor(rank[:, :, :, :], run[:, :, :, :], tot[:, :, :, :], ALU.subtract)
            dve.tensor_scalar(need[:, :], need[:, :], -1.0, float(KSEL), ALU.mult, ALU.add)
            dve.drain()
            dve.tensor_tensor(rank[:, :, :, :], rank[:, :, :, :], by_kind(PS[:, 6, 2 * P:4 * P]), ALU.add)
            dve.drain()
            need_b = need[:, :].unsqueeze(2).broadcast_to([P, E, NT])
            dve.tensor_tensor(sel[:, :, :], rank[:, 1, :, :], need_b, ALU.is_lt)
            dve.tensor_tensor(run[:, 1, :, :], rank[:, 1, :, :], need_b, ALU.min)
            dve.drain()
            dve.tensor_tensor(sel[:, :, :], sel[:, :, :], ge[:, 1, :, :], ALU.mult)
            dve.tensor_tensor(rank[:, 0, :, :], rank[:, 0, :, :], run[:, 1, :, :], ALU.add)
            dve.drain()
            dve.tensor_tensor(sel[:, :, :], sel[:, :, :], ge[:, 0, :, :], ALU.add)
            dve.drain()
            dve.scalar_tensor_tensor(slot[:, :, :], sel[:, :, :], -float(AWAY * LO), rank[:, 0, :, :], ALU.mult, ALU.add)
            dve.drain()
            dve.tensor_scalar(shi[:, :, :], slot[:, :, :], 4, None, ALU.arith_shift_right)
            dve.tensor_scalar(slo[:, :, :], slot[:, :, :], LO - 1, None, ALU.bitwise_and)
            dve.drain()
            dve.tensor_scalar(hib[:, :, :], shi[:, :, :], float(AWAY), None, ALU.add)
            dve.tensor_copy(lob[:, :, :], slo[:, :, :])
            dve.drain()
            for half in range(2):
                ts = slice(half * NT // 2, (half + 1) * NT // 2)
                for dst, part in ((ohl, lob), (ohh, hib)):
                    dve.tensor_tensor(dst[:, ts, :, :],
                                      iota_b[:, 0:LO].unsqueeze(1).unsqueeze(1).broadcast_to([P, NT // 2, E, LO]),
                                      part[:, :, ts].rearrange("p e t -> p t e").unsqueeze(3).broadcast_to([P, NT // 2, E, LO]),
                                      ALU.is_equal)
                dve.drain()
                low = ohl[:, ts, :, :].rearrange("p t e l -> p t (e l)")
                dve.tensor_scalar(ohv[:, ts, 0, :, :].rearrange("p t e l -> p t (e l)"), low, iota_pf[:, :], None, ALU.mult)
                for t in range(half * NT // 2, (half + 1) * NT // 2):
                    last = dve.tensor_scalar(ohv[:, t, 1, :, :].rearrange("p e l -> p (e l)"),
                                             ohl[:, t, :, :].rearrange("p e l -> p (e l)"), float(t), None, ALU.mult)
                last.then_inc(s_one_hots, 1)
            dve.wait_ge(s_slot_tokens, 1)
            dve.tensor_tensor(dm[:, :, :, :].rearrange("p v e l -> p v e l"),
                              PS[:, 4, 0:2 * E * LO].rearrange("p (v e l) -> p v e l", v=2, e=E),
                              of_expert[:, :].unsqueeze(1).unsqueeze(3).broadcast_to([P, 2, E, LO]), ALU.mult)
            dve.drain()
            dve.tensor_reduce(dv[:, :, :], dm[:, :, :, :].rearrange("p v e l -> p v l e"), AX_X, ALU.add)
            dve.drain()
            dve.scalar_tensor_tensor(tok[:, :], dv[:, 1, :], float(P), dv[:, 0, :], ALU.mult, ALU.add)
            dve.drain()
            dve.tensor_tensor(spread[:, :, :], tok[:, :].unsqueeze(1).broadcast_to([P, LOW_HI, LO]),
                              of_slot8[:, :].unsqueeze(2).broadcast_to([P, LOW_HI, LO]), ALU.mult).then_inc(s_slot_tokens_spread, 1)
            dve.wait_ge(s_index_product, 1)
            dve.tensor_copy(idx[:, :, :].rearrange("p e j -> p (e j)"), PS[:, 3, 0:E * SH]).then_inc(s_indices, 1)
            with dve.Fori(0, E // XP) as it:
                e = it * XP

                def take_probs(u):
                    dve.wait_ge(s_gathered_turned, e + (u + 1))
                    dve.tensor_copy(prob[u][:, :], xi[u][:, :, bass.ds(e + (DM + u), 1)].rearrange("p j o -> p (j o)")
                                    ).then_inc(s_row_probs, 1)

                def expert_out(u):
                    dve.wait_ge(s_w2_product, e + (u + 3))
                    dve.wait_ge(s_scattered, e * 32 + (u * 32 + CLEARED - 32))
                    dve.tensor_tensor(ost[u % 2][:, :, :], PS[:, u % 2, 0:SH * DM].rearrange("p (j d) -> p j d", j=SH),
                                      b2r[:, e + u, :].unsqueeze(1).broadcast_to([P, SH, DM]), ALU.add)
                    dve.drain()
                    for j in range(SH):
                        last = dve.tensor_scalar(ost[u % 2][:, j, :], ost[u % 2][:, j, :],
                                                 prob[u][:, j:j + 1], None, ALU.mult)
                    last.then_inc(s_expert_out, 1)

                take_probs(0)
                take_probs(1)
                take_probs(2)
                expert_out(0)
                take_probs(3)
                expert_out(1)
                expert_out(2)
                expert_out(3)

            def shift(c):
                dve.wait_ge(s_ln4_scales, c + 1)
                dve.scalar_tensor_tensor(nb5[:, c, :], mv5[:, c, :, 0], -1.0, rs5[:, c, :],
                                         ALU.mult, ALU.mult).then_inc(s_ln4_shifts, 1)

            for c in range(NC5):
                dve.wait_ge(s_ffn_sum_loaded[c], 16)
                layer_stats(lambda j: fin[:, c, j, :], mv5, c, s_ln4_stats)
                if c in (1, 2):
                    shift(c - 1)
            for c in range(NC5):
                if c in ACT5:
                    dve.wait_ge(s_ln4_normed, ACT5.index(c) + 1)
                else:
                    shift(3)
                    dve.wait_ge(s_ln4_scales, c + 1)
                    for j in range(CT):
                        dve.tensor_scalar(fin[:, c, j, :], fin[:, c, j, :], mv5[:, c, j, 0:1], rs5[:, c, j:j + 1],
                                          ALU.subtract, ALU.mult)
                    dve.drain()
                dve.tensor_tensor(res[:, c, :, :], fin[:, c, :, :], XA[:, c * CT:(c + 1) * CT, :], ALU.add).then_inc(s_result, 1)

        @block.tensor
        def _(pe):
            def warm_up(n):
                for _ in range(n):
                    pe.matmul(PS[:, 7, :], ones_b[:, :], ones_b[:, :].unsqueeze(1).broadcast_to([P, CH // P, P]),
                              start=True, stop=True)

            pe.sem_inc(s_y_summed, RING)
            pe.sem_inc(s_w2_product, 2)
            pe.wait_ge(s_constants, 1)
            warm_up(16)
            pe.wait_ge(s_identity_made, 1)
            def x_in(c):
                pe.wait_ge(s_normed, c + 1)
                for j in range(CT):
                    last = pe.transpose(PS[:, 2 * c, j * P:(j + 1) * P], xn[:, c, j, :], ident[:, :])
                last.then_inc(s_normed_turned, 1)
                pe.wait_ge(s_normed_t, c + 1)
                for h in range(H):
                    last = pe.matmul(PS[:, 2 * c + h, :], win[:, h * P:(h + 1) * P], xnT[:, c, :],
                                     start=True, stop=True)
                last.then_inc(s_x_in_product, 1)

            def z_product(c):
                pe.wait_ge(s_softplus_max, c + 1)
                for h in range(H):
                    last = pe.matmul(PS[:, 2 * c + h, :], win[:, DI + h * P:DI + (h + 1) * P], xnT[:, c, :],
                                     start=True, stop=True)
                last.then_inc(s_z_product, 1)

            def x_dbl(c):
                b, hc = divmod(c, HC)
                pe.wait_ge(s_x_conv, c + 1)
                pe.wait_ge(s_x_in, c + 1)
                for h in range(H):
                    last = pe.matmul(PS[0:XR, 2 * c, :], xpw[:, h, :], XC[:, b, h, hc * CH:(hc + 1) * CH],
                                     start=(h == 0), stop=(h == H - 1))
                last.then_inc(s_x_dbl_product, 1)

            def dt(c):
                pe.wait_ge(s_x_dbl, c + 1)
                for h in range(H):
                    last = pe.matmul(PS[:, 2 * c + h, :], dtw[:, h * P:(h + 1) * P], dbl[0:R, c, :],
                                     start=True, stop=True)
                last.then_inc(s_dt_product, 1)

            pe.wait_ge(s_in_weights_loaded, 32)
            x_in(0)
            x_in(1)
            pe.wait_ge(s_weights_loaded, 16 * NLOADS)
            pe.transpose(PS[:, 7, 0:NB1 + 6], vrows[:, :], ident[0:NB1 + 6, 0:NB1 + 6]).then_inc(s_vector_rows_turned, 1)
            x_in(2)
            x_dbl(0)
            pe.wait_ge(s_vector_columns, 1)
            x_in(3)
            dt(0)
            for c in range(1, NC):
                x_dbl(c)
                dt(c)
            for c in range(NC):
                z_product(c)
            pe.wait_ge(s_skip_diagonal, 1)
            for c in range(NC):
                b, hc = divmod(c, HC)
                pe.wait_ge(s_gate_silu, c + 1)
                for h in range(H):
                    pe.matmul(PS[:, 2 * c + h, :], diagd[:, h, :], XC[:, b, h, hc * CH:(hc + 1) * CH],
                              start=True, stop=False, skip_group_check=True)

            def sum_states(b, first, rings):
                with pe.Fori(0, rings) as it:
                    s = it * RING + first
                    for i in range(RING):
                        for h in range(H):
                            if h == 0:
                                pe.wait_ge(s_states_times_c_first_half, s + (b * NS + i + 1))
                            else:
                                pe.wait_ge(s_states_times_c, s + (b * NS + i + 1 + RING))
                            for hc in range(HC):
                                last = pe.matmul(PS[:, 2 * (b * HC + hc) + h, :], ident[:, :],
                                                 DB[:, i, h, hc * CH:(hc + 1) * CH], start=False, stop=False,
                                                 skip_group_check=True)
                        last.then_inc(s_y_summed, 1)

            def out_product(c):
                b, hc = divmod(c, HC)
                pe.wait_ge(s_y_gated, c + 1)
                for j in range(CT):
                    t = slice((hc * CT + j) * P, (hc * CT + j + 1) * P)
                    for h in range(H):
                        last = pe.matmul(PS[:, 2 * c, j * DM:(j + 1) * DM], SZ[:, b, h, t], outw[:, h, :],
                                         start=(h == 0), stop=(h == H - 1))
                last.then_inc(s_out_product, 1)

            def turn_normed(c):
                pe.wait_ge(s_hn, c + 1)
                for j in range(CT):
                    last = pe.transpose(PS[:, 2 * c + 1, j * P:(j + 1) * P], hn[:, c, j, :], ident[:, :])
                last.then_inc(s_hn_turned, 1)

            sum_states(0, 0, NS // RING)
            sum_states(1, 0, 1)
            out_product(0)
            out_product(1)
            sum_states(1, RING, NS // RING - 1)
            out_product(2)
            out_product(3)

            def fc(c):
                pe.wait_ge(s_hn_t, c + 1)
                for f in range(FH):
                    last = pe.matmul(PS[:, 2 * c + f, :], fcw[:, f * P:(f + 1) * P], hnT[:, c, :],
                                     start=True, stop=True)
                last.then_inc(s_fc_product, 1)

            def proj(c):
                pe.wait_ge(s_relu_squared, c + 1)
                for j in range(CT):
                    for f in range(FH):
                        last = pe.matmul(PS[:, 2 * c, j * DM:(j + 1) * DM], rel[:, c, f, j * P:(j + 1) * P],
                                         prw[:, f, :], start=(f == 0), stop=(f == FH - 1))
                last.then_inc(s_proj_product, 1)

            def turn_ffn_in(c):
                pe.wait_ge(*((s_ffn_in, c + 1) if c < NC - 1 else (s_ffn_in_last_chunk, 1)))
                for j in range(CT):
                    last = pe.transpose(PS[:, 2 * c + 1, j * P:(j + 1) * P], xb[:, c, j, :], ident[:, :])
                last.then_inc(s_ffn_in_turned, 1)

            def logits(c):
                pe.wait_ge(s_ffn_in_t, c + 1)
                for j in range(CT):
                    last = pe.matmul(PS[:, 2 * c, j * E:(j + 1) * E], xbT[:, c, j * P:(j + 1) * P], wsr[:, :],
                                     start=True, stop=True)
                last.then_inc(s_logit_product, 1)

            turn_normed(0)
            turn_normed(1)
            fc(0)
            fc(1)
            turn_normed(2)
            turn_normed(3)
            proj(0)
            fc(2)
            proj(1)
            fc(3)
            proj(2)
            proj(3)
            turn_ffn_in(0)
            for c in range(NC):
                if c + 1 < NC:
                    turn_ffn_in(c + 1)
                if c == 0:
                    warm_up(7)
                logits(c)
            pe.wait_ge(s_constants, 2)
            with pe.Fori(0, ROUNDS) as r:
                for t in range(NT):
                    if t % (NT // 2) == 0:
                        pe.wait_ge(s_counts, r * 2 + (1 + t // (NT // 2)))
                    last = pe.matmul(PS[:, 7, 0:NTHR * E], ones_b[:, :], reach[:, t, :, :].rearrange("p j e -> p (j e)"),
                                     start=(t == 0), stop=(t == NT - 1))
                last.then_inc(s_counts_summed, 1)
            pe.wait_ge(s_row_sums, 1)
            above_equal = ge[:, :, :, :].rearrange("p k e t -> p (k e t)")
            pe.matmul(PS[:, 6, 0:2 * P], ones_b[:, :], above_equal, start=True, stop=True)
            pe.matmul(PS[:, 6, 2 * P:4 * P], earlier[:, :], above_equal, start=True, stop=True).then_inc(s_rows_summed, 1)
            for t in range(NT):
                if t % (NT // 2) == 0:
                    pe.wait_ge(s_one_hots, 1 + t // (NT // 2))
                last = pe.matmul(PS[:, 4, 0:2 * E * LO], ohh[:, t, :, :].rearrange("p e h -> p (e h)"),
                                 ohv[:, t, :, :, :].rearrange("p v e l -> p (v e l)"), start=(t == 0), stop=(t == NT - 1))
            last.then_inc(s_slot_tokens, 1)
            pe.wait_ge(s_slot_tokens_spread, 1)
            pe.matmul(PS[:, 3, 0:E * SH], spread[:, :, :].rearrange("p a l -> p (a l)"),
                      of_half[:, :, :].rearrange("p e j -> p (e j)"), start=True, stop=True).then_inc(s_index_product, 1)
            warm_up(10)
            with pe.Fori(0, E // XP) as it:
                e = it * XP

                def turn(u):
                    pe.wait_ge(s_gathered[u], e * (32 // XP) + 32)
                    pe.wait_ge(s_gathered_t, e + (u + 1))
                    for j in range(SH):
                        last = pe.transpose(PS[:, 2 + u % 2, j * P:(j + 1) * P], xi[u][:, j, 0:DM], ident[:, :])
                    last.then_inc(s_gathered_turned, 1)

                def first_product(u):
                    pe.wait_ge(s_gathered_t, e + (u + 3))
                    pe.wait_ge(s_expert_weights[u], e * (32 // XP) + 32)
                    pe.wait_ge(s_gelu, e + (u + 1))
                    for k in range(FK):
                        last = pe.matmul(PS[:, 4 + 2 * (u % 2) + k // 2, (k % 2) * KSEL:(k % 2 + 1) * KSEL],
                                         w1s[:, u, k * P:(k + 1) * P], xiT[u % 2][:, :], start=True, stop=True)
                    last.then_inc(s_w1_product, 1)

                def second_product(u):
                    pe.wait_ge(s_gelu, e + (u + 3))
                    pe.wait_ge(s_expert_out, e + (u + 1))
                    for j in range(SH):
                        for k in range(FK):
                            last = pe.matmul(PS[:, u % 2, j * DM:(j + 1) * DM], hT[u % 2][:, k, j * P:(j + 1) * P],
                                             w2s[:, u, k, :], start=(k == 0), stop=(k == FK - 1))
                    last.then_inc(s_w2_product, 1)

                turn(0)
                first_product(0)
                turn(1)
                first_product(1)
                turn(2)
                second_product(0)
                first_product(2)
                turn(3)
                second_product(1)
                first_product(3)
                second_product(2)
                second_product(3)


_INS = ["x", "in_proj_w", "conv_w", "conv_b", "x_proj_w", "dt_proj_w", "dt_proj_b", "A_log", "D", "out_proj_w",
        "c_fc_w", "c_proj_w"]
_TURNED = {"in_proj_w", "x_proj_w", "dt_proj_w", "out_proj_w", "c_fc_w", "c_proj_w"}
_FFN = ["Ws", "bs", "W1", "b1", "W2", "b2"]


def kernel(**inputs):
    import numpy as _np
    import concourse.bacc as _bacc
    from concourse import mybir as _mybir
    from concourse.bass_utils import run_bass_kernel_spmd as _run

    nc = _bacc.Bacc("TRN2", target_bir_lowering=False, num_devices=1)
    arrays, args = {}, []
    for name in ["L0_attn_" + n for n in _INS] + ["L0_ffn_" + n for n in _FFN]:
        a = _np.asarray(inputs[name])
        if name.removeprefix("L0_attn_") in _TURNED:
            a = a.T
        a = _np.ascontiguousarray(a)
        arrays[f"in_{name}_dram"] = a
        args.append(nc.dram_tensor(f"in_{name}_dram", a.shape, _mybir.dt.from_np(a.dtype), kind="ExternalInput").ap())
    out = nc.dram_tensor("out_0_dram", inputs["L0_attn_x"].shape, _mybir.dt.float32, kind="ExternalOutput").ap()
    sandwich_kernel(nc, *args, out)
    r = _run(nc, [arrays], core_ids=[0])
    return r.results[0]["out_0_dram"]
```
